# Optimizing a Trainium2 kernel written in Bass

```python
import numpy as np
import jax
import jax.numpy as jnp

def _softmax(x, axis=-1):
    return jax.nn.softmax(x, axis=axis)

def _gelu(x):
    return jax.nn.gelu(x, approximate=True)

def _silu(x):
    return jax.nn.silu(x)

def _sigmoid(x):
    return jax.nn.sigmoid(x)

def _layernorm(x, axis=-1, eps=1e-05):
    m = jnp.mean(x, axis=axis, keepdims=True)
    v = jnp.var(x, axis=axis, keepdims=True)
    return (x - m) / jnp.sqrt(v + eps)

def _scatter_add(tgt, idx, src, axis=0):
    return tgt.at[idx].add(src)

def _segment_sum(src, seg, n):
    return jax.ops.segment_sum(src, seg, n)
kernel_name = 'mk_gnn_preln_d4_gnn_r32_975523'

def setup_inputs(seed: int=0):
    np.random.seed(seed)
    _w = jnp.asarray

    def _rec_inputs():
        import jax
        import jax.numpy as jnp
        _gk = jax.random.key(seed)
        x = -0.0001006 + 1 * jax.random.normal(jax.random.fold_in(_gk, 1), (3125, 96), jnp.float32)
        _s = jax.random.randint(jax.random.fold_in(_gk, 2), (25000,), 0, 3125, jnp.int32)
        _d = jax.random.randint(jax.random.fold_in(_gk, 3), (25000,), 0, 3125, jnp.int32)
        _loop = jnp.arange(3125, dtype=jnp.int32)
        src = jnp.concatenate([_s, _d, _loop])
        dst = jnp.concatenate([_d, _s, _loop])
        _o = jnp.argsort(dst, stable=True)
        src = src[_o]
        dst = dst[_o]
        edge_attr_32 = 0.000196303 + 1.00016 * jax.random.normal(jax.random.fold_in(_gk, 12), (53125, 32), jnp.float32)
        return (x, src, dst, edge_attr_32)
    x, src, dst, edge_attr_32 = _rec_inputs()

    def _L0_gnn_setup():
        import jax, jax.numpy as jnp
        import numpy as np
        N_NODES = 50000
        N_EDGES = 25000
        D_IN = 96
        D_OUT = 96
        K = 3
        LAMBDA_MAX = 2.0
        key = jax.random.key(seed)
        k1, k2, k3, k4, k5 = jax.random.split(key, 5)
        feat = jax.random.normal(k1, (N_NODES, D_IN), dtype=jnp.float32)
        scale = 1.0 / np.sqrt(K * D_IN)
        W = jax.random.uniform(k2, (K * D_IN, D_OUT), dtype=jnp.float32, minval=-scale, maxval=scale)
        b = jax.random.uniform(k3, (D_OUT,), dtype=jnp.float32, minval=-scale, maxval=scale)
        src = jax.random.randint(k4, (N_EDGES,), 0, N_NODES, dtype=jnp.int32)
        dst = jax.random.randint(k5, (N_EDGES,), 0, N_NODES, dtype=jnp.int32)
        return {'feat': feat, 'W': W, 'b': b, 'src': src, 'dst': dst}
    _L0_gnn_all = _L0_gnn_setup()
    _L0_gnn_in = {k: v for k, v in _L0_gnn_all.items() if k in ('W', 'b')}
    del _L0_gnn_all

    def _L1_gnn_setup():
        import jax, jax.numpy as jnp
        import numpy as np
        N, E = (50000, 25000)
        DIN = DOUT = 96
        DE = 32

        def _egnn_conv(x, src, dst, edge_attr, W_msg, W_edge, W_root, b):
            msg = x[src] @ W_msg + edge_attr @ W_edge
            agg = jax.ops.segment_max(msg, dst, num_segments=x.shape[0])
            agg = jnp.where(jnp.isneginf(agg), 0.0, agg)
            return agg + x @ W_root + b
        key = jax.random.key(seed)
        ks = jax.random.split(key, 10)
        rn = lambda k, sh, sc: jax.random.normal(k, sh, jnp.float32) * sc
        return {'X': rn(ks[0], (N, DIN), 1.0), 'edge_index': jax.random.randint(ks[1], (2, E), 0, N, jnp.int32), 'edge_attr': rn(ks[2], (E, DE), 1.0), 'W1_msg': rn(ks[3], (DIN, DOUT), DIN ** (-0.5)), 'W1_edge': rn(ks[4], (DE, DOUT), DE ** (-0.5)), 'W1_root': rn(ks[5], (DIN, DOUT), DIN ** (-0.5)), 'b1': jnp.zeros((DOUT,), jnp.float32), 'W2_msg': rn(ks[6], (DOUT, DOUT), DOUT ** (-0.5)), 'W2_edge': rn(ks[7], (DE, DOUT), DE ** (-0.5)), 'W2_root': rn(ks[8], (DOUT, DOUT), DOUT ** (-0.5)), 'b2': jnp.zeros((DOUT,), jnp.float32)}
    _L1_gnn_all = _L1_gnn_setup()
    _L1_gnn_in = {k: v for k, v in _L1_gnn_all.items() if k in ('W1_msg', 'W1_edge', 'W1_root', 'b1', 'W2_msg', 'W2_edge', 'W2_root', 'b2')}
    del _L1_gnn_all

    def _L2_gnn_setup():
        import jax, jax.numpy as jnp
        import numpy as np
        N_NODES = 50000
        N_FEAT = 96
        N_EDGES = 25000
        K_HOPS = 2
        key = jax.random.key(seed)
        k1, k2 = jax.random.split(key)
        x = jax.random.normal(k1, (N_NODES, N_FEAT), dtype=jnp.float32)
        edge_index = jax.random.randint(k2, (2, N_EDGES), 0, N_NODES, dtype=jnp.int64)
        return {'x': x, 'edge_index': edge_index}
    _L2_gnn_all = _L2_gnn_setup()
    _L2_gnn_in = {k: v for k, v in _L2_gnn_all.items() if k in ()}
    del _L2_gnn_all

    def _L3_gnn_setup():
        import jax, jax.numpy as jnp
        import numpy as np
        N_NODES = 50000
        N_EDGES = 25000
        D_IN = 96
        D_HID = 96
        D_OUT = 96

        def _mean_agg(x, src, dst, n_nodes):
            msg = x[src]
            summed = jax.ops.segment_sum(msg, dst, num_segments=n_nodes)
            deg = jax.ops.segment_sum(jnp.ones((src.shape[0],), x.dtype), dst, num_segments=n_nodes)
            return summed / jnp.maximum(deg, 1.0)[:, None]

        def _sage_conv(x, src, dst, W_self, W_neigh, b):
            agg = _mean_agg(x, src, dst, x.shape[0])
            return x @ W_self + agg @ W_neigh + b
        key = jax.random.key(seed)
        ks = jax.random.split(key, 9)
        s = 0.05
        return {'x': jax.random.normal(ks[0], (N_NODES, D_IN), jnp.float32), 'src': jax.random.randint(ks[1], (N_EDGES,), 0, N_NODES), 'dst': jax.random.randint(ks[2], (N_EDGES,), 0, N_NODES), 'W_self1': jax.random.normal(ks[3], (D_IN, D_HID), jnp.float32) * s, 'W_neigh1': jax.random.normal(ks[4], (D_IN, D_HID), jnp.float32) * s, 'b1': jnp.zeros((D_HID,), jnp.float32), 'W_self2': jax.random.normal(ks[5], (D_HID, D_OUT), jnp.float32) * s, 'W_neigh2': jax.random.normal(ks[6], (D_HID, D_OUT), jnp.float32) * s, 'b2': jnp.zeros((D_OUT,), jnp.float32)}
    _L3_gnn_all = _L3_gnn_setup()
    _L3_gnn_in = {k: v for k, v in _L3_gnn_all.items() if k in ('W_self1', 'W_neigh1', 'b1', 'W_self2', 'W_neigh2', 'b2')}
    del _L3_gnn_all
    return {'x': x, 'src': src, 'dst': dst, 'edge_attr_32': edge_attr_32, 'L0_gnn_W': _L0_gnn_in['W'], 'L0_gnn_b': _L0_gnn_in['b'], 'L1_gnn_W1_msg': _L1_gnn_in['W1_msg'], 'L1_gnn_W1_edge': _L1_gnn_in['W1_edge'], 'L1_gnn_W1_root': _L1_gnn_in['W1_root'], 'L1_gnn_b1': _L1_gnn_in['b1'], 'L1_gnn_W2_msg': _L1_gnn_in['W2_msg'], 'L1_gnn_W2_edge': _L1_gnn_in['W2_edge'], 'L1_gnn_W2_root': _L1_gnn_in['W2_root'], 'L1_gnn_b2': _L1_gnn_in['b2'], 'L3_gnn_W_self1': _L3_gnn_in['W_self1'], 'L3_gnn_W_neigh1': _L3_gnn_in['W_neigh1'], 'L3_gnn_b1': _L3_gnn_in['b1'], 'L3_gnn_W_self2': _L3_gnn_in['W_self2'], 'L3_gnn_W_neigh2': _L3_gnn_in['W_neigh2'], 'L3_gnn_b2': _L3_gnn_in['b2']}

def reference(x, src, dst, edge_attr_32, L0_gnn_W, L0_gnn_b, L1_gnn_W1_msg, L1_gnn_W1_edge, L1_gnn_W1_root, L1_gnn_b1, L1_gnn_W2_msg, L1_gnn_W2_edge, L1_gnn_W2_root, L1_gnn_b2, L3_gnn_W_self1, L3_gnn_W_neigh1, L3_gnn_b1, L3_gnn_W_self2, L3_gnn_W_neigh2, L3_gnn_b2):
    import jax
    import jax.numpy as jnp

    def _L0_gnn_ref(feat, W, b, src, dst):
        import jax, jax.numpy as jnp
        import numpy as np
        N_NODES = 50000
        N_EDGES = 25000
        D_IN = 96
        D_OUT = 96
        K = 3
        LAMBDA_MAX = 2.0
        n = feat.shape[0]
        deg = jax.ops.segment_sum(jnp.ones_like(dst, dtype=feat.dtype), dst, num_segments=n)
        D_invsqrt = jnp.clip(deg, 1.0, None) ** (-0.5)
        D_invsqrt = D_invsqrt[:, None]

        def unn_laplacian(x):
            h = (x * D_invsqrt)[src]
            agg = jax.ops.segment_sum(h, dst, num_segments=n)
            return agg * D_invsqrt
        re_norm = 2.0 / LAMBDA_MAX
        X0 = feat
        Xt = [X0]
        if K > 1:
            h = unn_laplacian(X0)
            X1 = -re_norm * h + X0 * (re_norm - 1.0)
            Xt.append(X1)
        for _ in range(2, K):
            h = unn_laplacian(X1)
            Xi = -2.0 * re_norm * h + X1 * (2.0 * (re_norm - 1.0)) - X0
            Xt.append(Xi)
            X1, X0 = (Xi, X1)
        Z = jnp.concatenate(Xt, axis=1)
        out = Z @ W + b
        return jax.nn.relu(out)

    def _L1_gnn_ref(X, edge_index, edge_attr, W1_msg, W1_edge, W1_root, b1, W2_msg, W2_edge, W2_root, b2):
        import jax, jax.numpy as jnp
        import numpy as np
        N, E = (50000, 25000)
        DIN = DOUT = 96
        DE = 32

        def _egnn_conv(x, src, dst, edge_attr, W_msg, W_edge, W_root, b):
            msg = x[src] @ W_msg + edge_attr @ W_edge
            agg = jax.ops.segment_max(msg, dst, num_segments=x.shape[0])
            agg = jnp.where(jnp.isneginf(agg), 0.0, agg)
            return agg + x @ W_root + b
        src, dst = (edge_index[0], edge_index[1])
        c1 = jax.nn.leaky_relu(_egnn_conv(X, src, dst, edge_attr, W1_msg, W1_edge, W1_root, b1))
        c2 = jax.nn.leaky_relu(_egnn_conv(c1, src, dst, edge_attr, W2_msg, W2_edge, W2_root, b2))
        return c2

    def _L2_gnn_ref(x, edge_index):
        import jax, jax.numpy as jnp
        import numpy as np
        N_NODES = 50000
        N_FEAT = 96
        N_EDGES = 25000
        K_HOPS = 2
        N = x.shape[0]
        loops = jnp.arange(N, dtype=edge_index.dtype)
        src = jnp.concatenate([edge_index[0], loops])
        dst = jnp.concatenate([edge_index[1], loops])
        ew = jnp.ones(src.shape[0], dtype=x.dtype)
        deg = jax.ops.segment_sum(ew, dst, num_segments=N)
        deg_inv_sqrt = jnp.where(deg > 0, jax.lax.rsqrt(deg), jnp.zeros_like(deg))
        norm = deg_inv_sqrt[src] * ew * deg_inv_sqrt[dst]

        def hop(h):
            return jax.ops.segment_sum(norm[:, None] * h[src], dst, num_segments=N)
        h = x
        for _ in range(K_HOPS):
            h = hop(h)
        return h

    def _L3_gnn_ref(x, src, dst, W_self1, W_neigh1, b1, W_self2, W_neigh2, b2):
        import jax, jax.numpy as jnp
        import numpy as np
        N_NODES = 50000
        N_EDGES = 25000
        D_IN = 96
        D_HID = 96
        D_OUT = 96

        def _mean_agg(x, src, dst, n_nodes):
            msg = x[src]
            summed = jax.ops.segment_sum(msg, dst, num_segments=n_nodes)
            deg = jax.ops.segment_sum(jnp.ones((src.shape[0],), x.dtype), dst, num_segments=n_nodes)
            return summed / jnp.maximum(deg, 1.0)[:, None]

        def _sage_conv(x, src, dst, W_self, W_neigh, b):
            agg = _mean_agg(x, src, dst, x.shape[0])
            return x @ W_self + agg @ W_neigh + b
        h = _sage_conv(x, src, dst, W_self1, W_neigh1, b1)
        h = jax.nn.relu(h)
        h = _sage_conv(h, src, dst, W_self2, W_neigh2, b2)
        return h
    edge_index = jnp.stack([src, dst])
    h = jnp.maximum(_layernorm(x, axis=-1), 0.0)
    x = x + _L0_gnn_ref(h, L0_gnn_W, L0_gnn_b, src, dst)
    h = jnp.maximum(_layernorm(x, axis=-1), 0.0)
    x = x + _L1_gnn_ref(h, edge_index, edge_attr_32, L1_gnn_W1_msg, L1_gnn_W1_edge, L1_gnn_W1_root, L1_gnn_b1, L1_gnn_W2_msg, L1_gnn_W2_edge, L1_gnn_W2_root, L1_gnn_b2)
    h = jnp.maximum(_layernorm(x, axis=-1), 0.0)
    x = x + _L2_gnn_ref(h, edge_index)
    h = jnp.maximum(_layernorm(x, axis=-1), 0.0)
    x = x + _L3_gnn_ref(h, src, dst, L3_gnn_W_self1, L3_gnn_W_neigh1, L3_gnn_b1, L3_gnn_W_self2, L3_gnn_W_neigh2, L3_gnn_b2)
    return x

_drawn_inputs = setup_inputs


def setup_inputs(seed=0):
    import zlib

    import numpy as np

    out = dict(_drawn_inputs(seed))
    spreads = {'L1_gnn_b1': (0.0, 0.293),
     'L1_gnn_b2': (0.0, 0.294),
     'L3_gnn_b1': (0.0, 0.8),
     'L3_gnn_b2': (0.0, 0.391)}
    factors = {'L0_gnn_b': 5.844}
    for name, (base, spread) in spreads.items():
        noise = np.random.default_rng([zlib.crc32(name.encode()), seed]).standard_normal(out[name].shape)
        drawn = base * np.exp(spread * noise) if base else spread * noise
        out[name] = jnp.asarray(drawn.astype(out[name].dtype))
    for name, factor in factors.items():
        out[name] = (out[name] * factor).astype(out[name].dtype)
    return out
```

```python
from contextlib import ExitStack

import concourse.bass as bass
from concourse import mybir

ALU = mybir.AluOpType
ACT = mybir.ActivationFunctionType
AX = mybir.AxisListType
F32 = mybir.dt.float32
F16 = mybir.dt.float16
I32 = mybir.dt.int32

P = 128
N = 3125
J = 25
PN = N // J
D = 96
DE = 32
E = 53125
T = 416
EP = P * T
WN = 5
WG = J // WN
WC = WN * J
AC = P * J * J
CH = 16
NCH = T // CH
Q = 4
NQ = CH // Q
HALF = CH // 2
BIG = 3.0e38
MAGIC = 12582912.0
LO = 2048.0
EPS = 1e-5
NO_DST = 4000
NO_KEY = 1.0e6


def gnn_kernel(nc, x, src, dst, ea, w0, b0, w1m, w1e, w1r, b1, w2m, w2e, w2r, b2,
               ws1, wn1, b31, ws2, wn2, b32, out):
    ctx = ExitStack()
    with ctx:
        def sb(name, shape, dt):
            return ctx.enter_context(nc.sbuf_tensor(name, shape, dt))

        def sem(name):
            return ctx.enter_context(nc.semaphore(name))

        dst_rows = nc.dram_tensor("dst_rows", [P, T], F32, kind="Internal").ap()
        keys_d = nc.dram_tensor("keys_d", [EP + P, 2], F32, kind="Internal").ap()
        ea_d = nc.dram_tensor("ea_d", [EP, DE], F32, kind="Internal").ap()
        y_d = [nc.dram_tensor(f"y_d{n}", [P * J, D], F32, kind="Internal").ap() for n in range(2)]
        run_d = [nc.dram_tensor(f"run_d{n}", [EP + P, D], F32, kind="Internal").ap() for n in range(2)]

        A = sb("A", [P, AC], F16)
        X = sb("X", [P, J, D], F32)
        H = sb("H", [P, J, D], F32)
        G = sb("G", [P, J, D], F32)
        HL = sb("HL", [P, J, 2 * D], F16)
        src_i = sb("src_i", [P, T + CH], I32)
        reset = sb("reset", [P, T], F32)
        ident = sb("ident", [P, P], F32)
        carry_reset = sb("carry_reset", [P, P], F32)
        wdense = sb("wdense", [D + 1, 4, D], F32)
        wedge = sb("wedge", [D + 1, 2, 2 * D], F32)
        wattr = sb("wattr", [P, 2, Q * D], F32)
        starts = sb("starts", [P, J + 1], F32)
        inv_sqrt_deg = sb("inv_sqrt_deg", [P, J], F32)
        inv_sqrt_deg1 = sb("inv_sqrt_deg1", [P, J], F32)
        inv_deg1 = sb("inv_deg1", [P, J], F32)
        inv_deg = sb("inv_deg", [P, J], F32)
        has_edges = sb("has_edges", [P, J], F32)
        end_i = sb("end_i", [P, J], I32)
        first_end_i = sb("first_end_i", [P, 1], I32)
        stat = sb("stat", [P, 3, J], F32)
        small = sb("small", [P, 6, J + 1], F32)
        idx_ring = sb("idx_ring", [P, CH], I32)
        row_i = sb("row_i", [P, J + 1], I32)
        win_i = sb("win_i", [P, WG], I32)

        A32 = A[:, :].bitcast(F32)
        found_rows = A32[:, 0:(J + 1) * T].rearrange("p (j t) -> p j t", j=J + 1)
        o = (J + 1) * T
        first_less = A32[:, o:o + (J + 1) * P].rearrange("p (j t) -> p j t", j=J + 1)
        o += (J + 1) * P
        window_keys = A32[:, o:o + WG * 2 * P].rearrange("p (g e k) -> p g e k", g=WG, k=2)
        o += WG * 2 * P
        row_trash = A32[:, o:o + T]
        o += T
        src_f = A32[:, o:o + T]
        o += T
        src_hi = A32[:, o:o + T]
        o += T
        node_id = A32[:, o:o + J + 1]
        o += J + 1
        part_edge = A32[:, o:o + 1]
        o += 1
        no_key = A32[:, o:o + 2]
        o += 2
        window_base = A32[:, o:o + WG * P]
        o += WG * P
        ones = A32[:, o:o + P]
        o += P
        diag = A32[:, o:o + 2 * P].rearrange("p (a b) -> p a b", a=2)
        o += 2 * P
        zero_rows = A32[:, o:o + D]
        o += D
        square0 = A32[:, o:o + J * D].rearrange("p (j d) -> p j d", d=D)
        G32 = G[:, :, :].rearrange("p j d -> p (j d)")
        HL32 = HL[:, :, :].rearrange("p j d -> p (j d)").bitcast(F32)
        dst_f = G32[:, 0:T]
        dst_i = G32[:, T:2 * T].bitcast(I32)
        keys = G32[:, 2 * T:4 * T].rearrange("p (t k) -> p t k", k=2)
        key_src = HL32[:, 0:WG * P]
        key_col = HL32[:, WG * P:2 * WG * P]
        onehot = HL32[:, 2 * WG * P:2 * WG * P + 8 * P].bitcast(F16).rearrange(
            "p (h w k c) -> p h w k c", h=2, w=4, k=2)
        iota16 = G32[:, 4 * T:4 * T + P // 2].bitcast(F16)
        XT = HL32[0:D + 1, 0:5 * 3 * P].rearrange("p (s m c) -> p s m c", s=5, m=3)
        gathered = HL32[:, 0:CH * D].rearrange("p (t d) -> p t d", d=D)
        o = CH * D
        attr = HL32[:, o:o + CH * DE].rearrange("p (h c) -> p h c", h=2)
        o += CH * DE
        attr_T = HL32[:, o:o + 2 * P].rearrange("p (h c) -> p h c", h=2)
        running = G32[:, 0:CH * D].rearrange("p (t d) -> p t d", d=D)
        o = CH * D
        carry_scan = G32[0:D, o:o + P + 1]
        o += P + 1
        first_seg = G32[:, o:o + D]
        o += D
        crossing = G32[:, o:o + D]
        agg = HL32.rearrange("p (j d) -> p j d", d=D)

        PS = [ctx.enter_context(nc.psum_tensor(f"ps{n}", [P, 512], F32)) for n in range(8)]

        s_const = sem("const_ready")
        s_pad = sem("edge_pads_set")
        s_padx = sem("node_pads_set")
        s_padw = sem("weight_pads_set")
        s_src = sem("src_loaded")
        s_dst = sem("dst_loaded")
        s_x = sem("x_loaded")
        s_ea0 = sem("edge_attr_pad_zero")
        s_ea = sem("edge_attr_copied")
        s_eap = sem("edge_attr_pad_stored")
        s_w0 = sem("dense_weights_loaded")
        s_w1 = sem("edge_weights_loaded")
        s_w3 = sem("last_weights_loaded")
        s_dstf = sem("dst_f_ready")
        s_keys = sem("keys_ready")
        s_rows_d = sem("dst_rows_stored")
        s_keys_d = sem("keys_stored")
        s_diag = sem("diag_ready")
        s_bcast = sem("bounds_broadcast")
        s_row_i = sem("row_index_ready")
        s_found = [sem("rows_found_window"), sem("rows_found_rest")]
        s_win_i = sem("window_index_ready")
        s_win = sem("window_keys_found")
        s_winT = sem("window_keys_transposed")
        s_onehot = sem("onehot_ready")
        s_amm = sem("adjacency_multiplied")
        s_aev = sem("adjacency_written")
        s_v = sem("vector_steps")
        s_a_in = sem("scalar_input")
        s_a_out = sem("scalar_output")
        s_split = sem("hop_operand_ready")
        s_hmm = sem("hop_multiplied")
        s_hlo = sem("hop_low_scaled")
        s_hsum = sem("hop_block_summed")
        s_din = sem("dense_input_ready")
        s_dT = sem("dense_transposed")
        s_dTc = sem("dense_transposed_copied")
        s_dmm = sem("dense_multiplied")
        s_dep = sem("dense_block_done")
        s_droot = sem("root_copied")
        s_y = sem("y_stored")
        s_idx = sem("gather_index_ready")
        s_turn = sem("gather_turns")
        s_gat = [sem(f"gathered{q}") for q in range(NQ)]
        s_attr = [sem(f"attr_loaded{h}") for h in range(2)]
        s_aT = sem("attr_transposed")
        s_aTc = sem("attr_transposed_copied")
        s_msg = sem("messages_ready")
        s_scan = sem("scanned")
        s_run = [sem(f"running_stored{h}") for h in range(2)]
        s_lastT = sem("last_state_transposed")
        s_carry = sem("carry_scanned")
        s_carryT = sem("carry_transposed")
        s_fs = sem("first_segment_found")
        s_cross = sem("crossing_ready")
        s_cross_d = sem("crossing_stored")
        s_agg = sem("aggregates_found")
        s_aggu = sem("aggregates_used")
        s_out = sem("out_stored")

        block = ctx.enter_context(nc.Block())

        DENSE = [(3, D), (1, 2 * D), (1, 2 * D), (2, D), (2, D)]

        @block.sync
        def _(sp):
            full = (P - 1) * T
            sp.wait_ge(s_pad, 2)
            for edge, tile, done in ((dst, dst_i, s_dst), (src, src_i, s_src)):
                for a, b in ((0, 112), (112, P - 1)):
                    sp.dma_start(tile[a:b, 0:T], edge[a * T:b * T].rearrange("(p t) -> p t", t=T)).then_inc(done, 16)
                sp.dma_start(tile[P - 1:P, 0:E - full], edge[full:E].rearrange("(p t) -> p t", p=1)).then_inc(done, 16)
            sp.wait_ge(s_padx, 1)
            for a, b in ((0, 112), (112, PN)):
                sp.dma_start(X[a:b, :, :], x[a * J:b * J, :].rearrange("(p j) d -> p j d", j=J)).then_inc(s_x, 16)
            sp.wait_ge(s_dstf, 1)
            sp.dma_start(dst_rows, dst_f).then_inc(s_rows_d, 16)
            sp.wait_ge(s_padw, 1)
            sp.dma_start(wdense[0:D, 0:3, :], w0.rearrange("(k d) n -> d k n", d=D)).then_inc(s_w0, 16)
            sp.dma_start(wdense[D:D + 1, 0, :], b0.rearrange("(a n) -> a n", a=1)).then_inc(s_w0, 16)
            for n, (wm, wr, b, we) in enumerate(((w1m, w1r, b1, w1e), (w2m, w2r, b2, w2e))):
                sp.dma_start(wedge[0:D, n, 0:D], wm).then_inc(s_w1, 16)
                sp.dma_start(wedge[0:D, n, D:2 * D], wr).then_inc(s_w1, 16)
                sp.dma_start(wedge[D:D + 1, n, D:2 * D], b.rearrange("(a n) -> a n", a=1)).then_inc(s_w1, 16)
                for q in range(Q):
                    sp.dma_start(wattr[q * DE:(q + 1) * DE, n, q * D:(q + 1) * D], we).then_inc(s_w1, 16)
            sp.wait_ge(s_keys, 1)
            sp.dma_start(keys_d[0:EP, :].rearrange("(p t) k -> p t k", t=T), keys).then_inc(s_keys_d, 16)
            sp.dma_start(keys_d[EP:EP + P, :], no_key).then_inc(s_keys_d, 16)
            sp.dma_start(ea_d[0:E, :].rearrange("(a b c) d -> a b (c d)", a=25, b=17),
                         ea.rearrange("(a b c) d -> a b (c d)", a=25, b=17)).then_inc(s_ea, 16)
            sp.wait_ge(s_ea0, 1)
            sp.dma_start(ea_d[E:EP, :], zero_rows[0:EP - E, 0:DE]).then_inc(s_eap, 16)
            for n in range(2):
                sp.dma_start(run_d[n][EP:EP + P, :], zero_rows).then_inc(s_run[n], 16)

            sp.wait_ge(s_dep, 5 + J)
            for a, b in ((0, 112), (112, PN)):
                sp.dma_start(G[a:b, :, :], x[a * J:b * J, :].rearrange("(p j) d -> p j d", j=J)).then_inc(s_x, 16)

            ea_t = ea_d.rearrange("(p t) d -> p (t d)", t=T)
            for n in range(2):
                sp.wait_ge(s_dep, 5 + J * (n + 2))
                for a, b in ((0, 64), (64, P)):
                    sp.dma_start(y_d[n].rearrange("(p j) d -> p j d", j=J)[a:b], G[a:b, :, :]).then_inc(s_y, 16)
                if n == 0:
                    sp.wait_ge(s_ea, 16)
                    sp.wait_ge(s_eap, 16)
                run_t = run_d[n][0:EP, :].rearrange("(p t) d -> p (t d)", t=T)
                hw = HALF * DE
                sp.wait_ge(s_aT, 4 + n * NCH * NQ)
                for h in range(2):
                    sp.dma_start(attr[:, h, :], ea_t[:, h * hw:(h + 1) * hw]).then_inc(s_attr[h], 16)

                def store(it, h):
                    sp.wait_ge(s_scan, it * CH + (CH + n * T + (h + 1) * HALF))
                    sp.dma_start(run_t[:, bass.ds(it * (CH * D) + h * HALF * D, HALF * D)],
                                 running[:, h * HALF:(h + 1) * HALF, :].rearrange("p t d -> p (t d)")
                                 ).then_inc(s_run[h], 16)

                with sp.Fori(0, NCH - 1) as it:
                    for h in range(2):
                        sp.wait_ge(s_aT, it * NQ + (4 + n * NCH * NQ + 2 * (h + 1)))
                        sp.dma_start(attr[:, h, :], ea_t[:, bass.ds(it * (CH * DE) + CH * DE + h * hw, hw)]
                                     ).then_inc(s_attr[h], 16)
                        store(it, h)
                for h in range(2):
                    store(NCH - 1, h)
                sp.wait_ge(s_cross, n + 1)
                sp.dma_start(run_d[n][EP:EP + P, :], crossing).then_inc(s_cross_d, 16)
                if n == 0:
                    for m, w in enumerate((ws1, wn1, ws2, wn2)):
                        sp.dma_start(wdense[0:D, m, :], w).then_inc(s_w3, 16)
                    for m, b in ((0, b31), (2, b32)):
                        sp.dma_start(wdense[D:D + 1, m, :], b.rearrange("(a n) -> a n", a=1)).then_inc(s_w3, 16)
            sp.wait_ge(s_dep, 5 + J * 5)
            for a, b in ((0, 112), (112, PN)):
                sp.dma_start(out[a * J:b * J, :].rearrange("(p j) d -> p j d", j=J), X[a:b, :, :]).then_inc(s_out, 16)
            sp.wait_ge(s_out, 32)

        @block.gpsimd
        def _(pool):
            pool.memset(src_i[:, :], 0).then_inc(s_pad, 1)
            pool.memset(dst_i, NO_DST).then_inc(s_pad, 1)
            pool.memset(wdense[:, :, :], 0.0)
            pool.memset(wedge[:, :, :], 0.0)
            pool.memset(wattr[:, :, :], 0.0).then_inc(s_padw, 1)
            pool.memset(zero_rows, 0.0).then_inc(s_ea0, 1)
            pool.memset(ones, 1.0)
            pool.memset(no_key, NO_KEY)
            pool.iota(node_id, [[1, J + 1]], base=0, channel_multiplier=J, allow_small_or_imprecise_dtypes=True)
            pool.iota(part_edge, [[0, 1]], base=0, channel_multiplier=T, allow_small_or_imprecise_dtypes=True)
            pool.iota(window_base, [[WC, WG], [J * J, P]], base=0, channel_multiplier=0,
                      allow_small_or_imprecise_dtypes=True)
            pool.iota(iota16, [[1, P]], base=0, channel_multiplier=0, allow_small_or_imprecise_dtypes=True)
            pool.memset(ident[:, :], 0.0).then_inc(s_const, 1)
            pool.wait_ge(s_const, 1)
            pool.affine_select(out=ident[:, :], in_=ident[:, :], compare_op=ALU.not_equal, fill=1.0, base=0,
                               pattern=[[-1, P]], channel_multiplier=1).then_inc(s_const, 1)

            def gather(dest, table, index):
                return pool.indirect_dma_start(out=dest, out_offset=None, in_=table,
                                               in_offset=bass.IndirectOffsetOnAxis(ap=index, axis=0))

            pool.wait_ge(s_row_i, 1)
            pool.wait_ge(s_rows_d, 16)
            first = list(range(0, J + 1, WN))
            for j in first:
                gather(found_rows[:, j, :], dst_rows, row_i[:, j:j + 1]).then_inc(s_found[0], 16)
            pool.wait_ge(s_win_i, 1)
            pool.wait_ge(s_keys_d, 32)
            for g in range(WG):
                gather(window_keys[:, g, :, :].rearrange("p e k -> p (e k)"), keys_d,
                       win_i[:, g:g + 1]).then_inc(s_win, 16)
            for j in range(J + 1):
                if j not in first:
                    gather(found_rows[:, j, :], dst_rows, row_i[:, j:j + 1]).then_inc(s_found[1], 16)

            for n in range(2):
                pool.wait_ge(s_y, 32 * (n + 1))
                with pool.Fori(0, NCH) as it:
                    for q in range(NQ):
                        pool.wait_ge(s_idx, it * NQ + (n * (NCH + 1) * NQ + q + 1))
                        pool.sem_inc(s_turn, 1)
                        for t in range(q * Q, (q + 1) * Q):
                            gather(gathered[:, t, :], y_d[n], idx_ring[:, t:t + 1]).then_inc(s_gat[q], 16)
                for h in range(2):
                    pool.wait_ge(s_run[h], 16 * (NCH * (n + 1) + 1))
                gather(first_seg, run_d[n], first_end_i[:, 0:1]).then_inc(s_fs, 16)
                pool.wait_ge(s_cross_d, 16 * (n + 1))
                for j in range(J):
                    gather(agg[:, j, :], run_d[n], end_i[:, j:j + 1]).then_inc(s_agg, 16)

        @block.tensor
        def _(pe):
            pe.wait_ge(s_const, 2)
            pe.wait_ge(s_diag, 1)
            for m in range(2):
                mm = pe.matmul(PS[7][:, m * P:(m + 1) * P], ones, diag[:, m, :], start=True, stop=True)
            mm.then_inc(s_bcast, 1)
            pe.wait_ge(s_win, 16 * WG)
            for m in range(2 * WG):
                k, g = divmod(m, WG)
                mm = pe.transpose(PS[m // 4][:, (m % 4) * P:(m % 4 + 1) * P], window_keys[:, g, :, k], ident[:, :])
            mm.then_inc(s_winT, 1)
            with pe.Fori(0, WG * P // 8) as it:
                for h in range(2):
                    pe.wait_ge(s_onehot, it * 2 + (h + 1))
                    pe.wait_ge(s_aev, it * 2 + (h + 1))
                    for w in range(4):
                        mm = pe.matmul(PS[4 + h][:, w * WC:(w + 1) * WC], onehot[:, h, w, 0, :],
                                       onehot[:, h, w, 1, 0:WC], start=True, stop=True)
                    mm.then_inc(s_amm, 1)

            def hop(k):
                pe.wait_ge(s_split, k + 1)
                if k == 0:
                    pe.wait_ge(s_aev, 2 + WG * P // 4)
                with pe.Fori(0, J // 5) as it:
                    for b in range(5):
                        pe.wait_ge(s_hsum, it * 5 + (J * k + b + 1))
                        for j in range(J):
                            mm = pe.matmul(PS[b][:, 0:2 * D],
                                           A[:, bass.ds(it * (5 * J) + b * J + j, P, step=J * J)],
                                           HL[:, j, :], start=(j == 0), stop=(j == J - 1))
                        mm.then_inc(s_hmm, 1)

            def dense(k, inputs, weights):
                m, w = DENSE[k]
                pe.wait_ge(s_din, k + 1)

                def turn(b):
                    for i, blocks in enumerate(inputs):
                        tr = pe.transpose(PS[5 + b % 5 % 3][0:D, i * P:(i + 1) * P], blocks[:, b, :], ident[:, :])
                    tr.then_inc(s_dT, 1)

                turn(0)
                for b in range(J):
                    if b < J - 1:
                        turn(b + 1)
                    pe.wait_ge(s_dTc, J * k + b + 1)
                    pe.wait_ge(s_dep, J * k + b + 1)
                    for i in range(m):
                        rows = D + 1 if i == 0 else D
                        mm = pe.matmul(PS[b % 5][:, 0:w], XT[0:rows, b % 5, i, :], weights[i][0:rows],
                                       start=(i == 0), stop=(i == m - 1))
                    mm.then_inc(s_dmm, 1)

            def edges(n):
                with pe.Fori(0, NCH) as it:
                    def turn(q):
                        if q % 2 == 0:
                            pe.wait_ge(s_attr[q // 2], it * 16 + 16 * (n * NCH + 1))
                        pe.wait_ge(s_aTc, it * NQ + (n * NCH * NQ + q + 1))
                        pe.transpose(PS[4 + q % 2][:, 0:P], attr[:, q // 2, (q % 2) * P:(q % 2 + 1) * P],
                                     ident[:, :]).then_inc(s_aT, 1)

                    turn(0)
                    for q in range(NQ):
                        if q < NQ - 1:
                            turn(q + 1)
                        pe.wait_ge(s_aTc, it * NQ + (n * NCH * NQ + q + 1 + 2))
                        pe.wait_ge(s_scan, it * CH + (n * T + (q + 1) * Q))
                        pe.matmul(PS[q][:, 0:Q * D], attr_T[:, q % 2, :], wattr[:, n, :], start=True, stop=False)
                        pe.wait_ge(s_gat[q], it * (16 * Q) + 16 * Q * (n * NCH + 1))
                        pe.matmul(PS[q][:, 0:Q * D], ident[:, :],
                                  gathered[:, q * Q:(q + 1) * Q, :].rearrange("p t d -> p (t d)"),
                                  start=False, stop=True).then_inc(s_msg, 1)
                pe.wait_ge(s_scan, CH + (n + 1) * T)
                pe.transpose(PS[6][0:D, 0:P], running[:, CH - 1, :], ident[:, :]).then_inc(s_lastT, 1)
                pe.wait_ge(s_carry, n + 1)
                pe.transpose(PS[7][:, 0:D], carry_scan[:, 0:P], ident[0:D, 0:D]).then_inc(s_carryT, 1)

            hop(0)
            hop(1)
            pe.wait_ge(s_w0, 32)
            dense(0, (H, X, G), [wdense[:, m, :] for m in range(3)])
            pe.wait_ge(s_w1, 14 * 16)
            dense(1, (H,), [wedge[:, 0, :]])
            edges(0)
            dense(2, (H,), [wedge[:, 1, :]])
            edges(1)
            hop(2)
            hop(3)
            hop(4)
            pe.wait_ge(s_w3, 6 * 16)
            dense(3, (H, G), [wdense[:, 0, :], wdense[:, 1, :]])
            hop(5)
            dense(4, (H, G), [wdense[:, 2, :], wdense[:, 3, :]])

        @block.scalar
        def _(act):
            asked = [0]

            def on_request(out_, in_, func, scale=1.0):
                asked[0] += 1
                act.wait_ge(s_a_in, asked[0])
                act.activation(out_, in_, func, scale=scale).then_inc(s_a_out, 1)

            def layernorm(square):
                on_request(square, H[:, :, :], ACT.Square)
                on_request(stat[:, 2, :], stat[:, 1, :], ACT.Sqrt)

            def split(source):
                on_request(HL[:, :, 0:D], source, ACT.Copy)
                asked[0] += 1
                act.wait_ge(s_a_in, asked[0])
                act.activation(HL[:, :, D:2 * D], G[:, :, :], ACT.Copy, scale=LO).then_inc(s_split, 1)

            def hop(k):
                with act.Fori(0, J // 5) as it:
                    for b in range(5):
                        act.wait_ge(s_hmm, it * 5 + (J * k + b + 1))
                        act.activation(G[:, bass.ds(it * 5 + b, 1), :].rearrange("p a d -> p (a d)"),
                                       PS[b][:, D:2 * D], ACT.Copy, scale=1.0 / LO).then_inc(s_hlo, 1)

            def dense(k, root=False):
                m, w = DENSE[k]
                with act.Fori(0, J // 5) as it:
                    for b in range(5):
                        act.wait_ge(s_dT, it * 5 + (J * k + b + 1))
                        act.activation(XT[0:D, b, 0:m, :], PS[5 + b % 3][0:D, 0:m * P].rearrange(
                            "p (m c) -> p m c", m=m), ACT.Copy).then_inc(s_dTc, 1)
                        if root:
                            act.wait_ge(s_dmm, it * 5 + (J * k + b + 1))
                            act.activation(H[:, bass.ds(it * 5 + b, 1), :].rearrange("p a d -> p (a d)"),
                                           PS[b][:, D:2 * D], ACT.Copy).then_inc(s_droot, 1)

            def edges(n):
                def index(q, it):
                    act.activation(idx_ring[:, q * Q:(q + 1) * Q], src_i[:, bass.ds(it * CH + q * Q, Q)],
                                   ACT.Copy).then_inc(s_idx, 1)

                for q in range(NQ):
                    index(q, 0)
                with act.Fori(0, NCH) as it:
                    for q in range(NQ):
                        act.wait_ge(s_aT, it * NQ + (4 + n * NCH * NQ + q + 1))
                        act.wait_ge(s_msg, it * NQ + (n * NCH * NQ + q + 1))
                        act.activation(attr_T[:, q % 2, :], PS[4 + q % 2][:, 0:P], ACT.Copy).then_inc(s_aTc, 1)
                        act.wait_ge(s_msg, it * NQ + (n * NCH * NQ + q + 1 + 2))
                        index(q, it + 1)

            act.wait_ge(s_x, 32)
            layernorm(square0)
            on_request(small[:, 3, 0:J], small[:, 2, 0:J], ACT.Sqrt)
            on_request(small[:, 5, 0:J], small[:, 4, 0:J], ACT.Sqrt)
            act.wait_ge(s_eap, 16)
            act.wait_ge(s_keys_d, 32)
            for h in range(2):
                act.wait_ge(s_run[h], 16)
            with act.Fori(0, WG) as g:
                with act.Fori(0, P // 8) as i8:
                    for h in range(2):
                        act.wait_ge(s_amm, g * (P // 4) + i8 * 2 + (2 + h + 1))
                        act.activation(
                            A[:, :].rearrange("p (w c) -> p w c", c=J * J)[
                                :, bass.ds(i8 * 8 + h * 4, 4), bass.ds(g * WC, WC)],
                            PS[4 + h][:, 0:4 * WC].rearrange("p (w c) -> p w c", w=4), ACT.Copy).then_inc(s_aev, 1)
            split(G[:, :, :])
            hop(0)
            split(G[:, :, :])
            hop(1)
            dense(0)
            layernorm(G[:, :, :])
            dense(1, root=True)
            edges(0)
            dense(2, root=True)
            edges(1)
            layernorm(G[:, :, :])
            split(G[:, :, :])
            hop(2)
            split(G[:, :, :])
            hop(3)
            layernorm(G[:, :, :])
            split(H[:, :, :])
            hop(4)
            dense(3)
            split(H[:, :, :])
            hop(5)
            dense(4)

        @block.vector
        def _(dve):
            steps = [0]
            asks = [0]

            def v(instruction):
                steps[0] += 1
                instruction.then_inc(s_v, 1)
                dve.wait_ge(s_v, steps[0])

            def ask(instruction):
                asks[0] += 1
                instruction.then_inc(s_a_in, 1)
                dve.wait_ge(s_a_in, asks[0])

            answers = [0]

            def answer():
                answers[0] += 1
                dve.wait_ge(s_a_out, answers[0])

            def per_node(t):
                return t.unsqueeze(2).to_broadcast([P, J, D])

            def magic(t):
                v(dve.tensor_scalar(t, t, MAGIC, MAGIC, ALU.add, ALU.subtract))

            def layernorm(square):
                v(dve.tensor_reduce(stat[:, 0, :], X[:, :, :], AX.X, ALU.add))
                v(dve.tensor_scalar(stat[:, 0, :], stat[:, 0, :], 1.0 / D, None, ALU.mult))
                ask(dve.tensor_tensor(H[:, :, :], X[:, :, :], per_node(stat[:, 0, :]), ALU.subtract))
                answer()
                v(dve.tensor_reduce(stat[:, 1, :], square, AX.X, ALU.add))
                ask(dve.tensor_scalar(stat[:, 1, :], stat[:, 1, :], 1.0 / D, EPS, ALU.mult, ALU.add))
                answer()
                v(dve.reciprocal(stat[:, 0, :], stat[:, 2, :]))
                v(dve.scalar_tensor_tensor(H[:, :, :], H[:, :, :], 0.0, per_node(stat[:, 0, :]), ALU.max, ALU.mult))

            def scale(out_, in_, by):
                return dve.tensor_tensor(out_, in_, per_node(by[:, 0:J]), ALU.mult)

            def split(source, last):
                ask(last)
                answer()
                asks[0] += 1
                dve.tensor_tensor(G[:, :, :], source, HL[:, :, 0:D], ALU.subtract).then_inc(s_a_in, 1)

            def hop(k):
                with dve.Fori(0, J // 5) as it:
                    for b in range(5):
                        dve.wait_ge(s_hlo, it * 5 + (J * k + b + 1))
                        g = G[:, bass.ds(it * 5 + b, 1), :].rearrange("p a d -> p (a d)")
                        dve.tensor_tensor(g, PS[b][:, 0:D], g, ALU.add).then_inc(s_hsum, 1)
                dve.wait_ge(s_hsum, 5 + J * (k + 1))

            def dense(k, last, finish):
                last.then_inc(s_din, 1)
                m, w = DENSE[k]
                with dve.Fori(0, J // 5) as it:
                    for b in range(5):
                        dve.wait_ge(s_dmm, it * 5 + (J * k + b + 1))
                        if w > D:
                            dve.wait_ge(s_droot, it * 5 + (J * (k - 1) + b + 1))
                        at = bass.ds(it * 5 + b, 1)
                        finish(PS[b][:, 0:D], at).then_inc(s_dep, 1)
                dve.wait_ge(s_dep, 5 + J * (k + 1))

            def rows(t, at):
                return t[:, at, :].rearrange("p a d -> p (a d)")

            def edges(n):
                v(dve.memset(running[:, CH - 1, :], -BIG))
                v(dve.memset(carry_scan[:, 0:1], -BIG))
                with dve.Fori(0, NCH) as it:
                    for q in range(NQ):
                        dve.wait_ge(s_msg, it * NQ + (n * NCH * NQ + q + 1 + 2))
                        if q % 2 == 0:
                            dve.wait_ge(s_run[q // 2], it * 16 + 16 * (n * NCH + 1))
                        for i in range(Q):
                            t = q * Q + i
                            dve.wait_ge(s_scan, it * CH + (CH + n * T + t))
                            dve.scalar_tensor_tensor(running[:, t, :], running[:, (t - 1) % CH, :],
                                                     reset[:, bass.ds(it * CH + t, 1)],
                                                     PS[q][:, i * D:(i + 1) * D], ALU.add, ALU.max
                                                     ).then_inc(s_scan, 1)
                dve.wait_ge(s_lastT, n + 1)
                dve.tensor_tensor_scan(carry_scan[:, 1:P + 1], carry_reset[0:D, :], PS[6][0:D, 0:P], -BIG,
                                       ALU.add, ALU.max).then_inc(s_carry, 1)
                dve.wait_ge(s_carryT, n + 1)
                dve.wait_ge(s_fs, 16 * (n + 1))
                dve.tensor_tensor(crossing, PS[7][:, 0:D], first_seg, ALU.max).then_inc(s_cross, 1)
                dve.wait_ge(s_agg, 16 * J * (n + 1))
                v(scale(agg, agg, has_edges))
                v(dve.tensor_tensor(agg, agg, H[:, :, :], ALU.add))

            def leaky(out_):
                return dve.scalar_tensor_tensor(out_, agg, 0.01, agg, ALU.mult, ALU.max)

            for signal, count in ((s_aev, 2), (s_amm, 2), (s_hsum, 5), (s_dep, 5), (s_scan, CH), (s_aT, 4),
                                  (s_aTc, 2), (s_msg, 2)):
                dve.sem_inc(signal, count)
            dve.memset(X[:, :, :], 0.0).then_inc(s_padx, 1)

            dve.wait_ge(s_dst, 48)
            v(dve.tensor_copy(dst_f, dst_i))
            dve.tensor_copy(dst_f[:, 0:1], dst_i[:, 0:1]).then_inc(s_dstf, 1)
            dve.wait_ge(s_const, 2)
            dve.wait_ge(s_dstf, 1)
            dve.tensor_scalar(diag[:, 0, :], ident[:, :], dst_f[:, 0:1], None, ALU.mult)
            dve.tensor_scalar(diag[:, 1, :], ident[:, :], dst_f[:, T - 1:T], None, ALU.mult).then_inc(s_diag, 1)
            dve.wait_ge(s_bcast, 1)
            v(dve.tensor_tensor(first_less, PS[7][:, 0:P].unsqueeze(1).to_broadcast([P, J + 1, P]),
                                node_id.unsqueeze(2).to_broadcast([P, J + 1, P]), ALU.is_lt))
            v(dve.tensor_reduce(small[:, 0, :], first_less, AX.X, ALU.add))
            v(dve.tensor_scalar(small[:, 0, :], small[:, 0, :], 1.0, 0.0, ALU.subtract, ALU.max))
            dve.tensor_copy(row_i[:, :], small[:, 0, :]).then_inc(s_row_i, 1)
            dve.wait_ge(s_src, 48)
            v(dve.tensor_copy(src_f, src_i[:, 0:T]))
            v(dve.tensor_scalar(src_hi, src_f, 1.0 / J, 0.48, ALU.mult, ALU.subtract))
            magic(src_hi)
            v(dve.scalar_tensor_tensor(src_f, src_hi, -float(J), src_f, ALU.mult, ALU.add))
            dve.tensor_copy(keys[:, :, 0], src_hi)
            dve.scalar_tensor_tensor(keys[:, :, 1], dst_f, float(J), src_f, ALU.mult, ALU.add).then_inc(s_keys, 1)

            def count(j):
                v(dve.tensor_scalar(row_trash, found_rows[:, j, :], node_id[:, j:j + 1], None, ALU.is_lt, ALU.add,
                                    accum_out=small[:, 1, j:j + 1]))
                v(dve.scalar_tensor_tensor(starts[:, j:j + 1], small[:, 0, j:j + 1], float(T),
                                           small[:, 1, j:j + 1], ALU.mult, ALU.add))

            dve.wait_ge(s_found[0], 16 * (WG + 1))
            for j in range(0, J + 1, WN):
                count(j)
            dve.tensor_copy(win_i[:, :], starts[:, 0:J:WN]).then_inc(s_win_i, 1)

            v(dve.memset(reset[:, 0:1], 0.0))
            v(dve.tensor_tensor(reset[:, 1:T], dst_f[:, 1:T], dst_f[:, 0:T - 1], ALU.not_equal))
            v(dve.tensor_scalar(reset[:, :], reset[:, :], -BIG, None, ALU.mult))
            v(dve.memset(carry_reset[:, 0:1], -BIG))
            v(dve.tensor_copy(diag[:, 1, :], PS[7][:, P:2 * P]))
            v(dve.tensor_tensor(carry_reset[:, 1:P], diag[:, 1, 1:P], diag[:, 1, 0:P - 1], ALU.not_equal))
            v(dve.tensor_scalar(carry_reset[:, 1:P], carry_reset[:, 1:P], -BIG, None, ALU.mult))
            v(dve.tensor_scalar(row_trash, dst_f, dst_f[:, 0:1], None, ALU.is_equal, ALU.add,
                                accum_out=small[:, 1, 1:2]))
            v(dve.scalar_tensor_tensor(small[:, 1, 1:2], small[:, 1, 1:2], -1.0, part_edge, ALU.add, ALU.add))
            v(dve.tensor_copy(first_end_i[:, :], small[:, 1, 1:2]))

            dve.wait_ge(s_x, 32)
            layernorm(square0)

            dve.wait_ge(s_winT, 1)
            for b in range(3):
                lo, hi = b * 4, min(b * 4 + 4, 2 * WG)
                cut = min(max(WG - lo, 0), 4)
                if cut:
                    v(dve.tensor_copy(key_src[:, lo * P:(lo + cut) * P], PS[b][:, 0:cut * P]))
                if lo + cut < hi:
                    a = (lo + cut - WG) * P
                    z = (hi - WG) * P
                    v(dve.tensor_tensor(key_col[:, a:z], PS[b][:, cut * P:(hi - lo) * P], window_base[:, a:z],
                                        ALU.subtract))
            dve.wait_ge(s_found[1], 16 * (J + 1 - WG - 1))
            for j in range(J + 1):
                if j % WN:
                    count(j)
            deg = small[:, 1, 0:J]
            v(dve.tensor_tensor(deg, starts[:, 1:J + 1], starts[:, 0:J], ALU.subtract))
            v(dve.tensor_scalar(has_edges[:, :], deg, 1.0, None, ALU.min))
            v(dve.tensor_scalar(small[:, 4, 0:J], deg, 1.0, None, ALU.add))
            v(dve.reciprocal(inv_deg1[:, :], small[:, 4, 0:J]))
            ask(dve.tensor_scalar(small[:, 2, 0:J], deg, 1.0, None, ALU.max))
            answer()
            v(dve.reciprocal(inv_sqrt_deg[:, :], small[:, 3, 0:J]))
            ask(dve.reciprocal(inv_deg[:, :], small[:, 2, 0:J]))
            answer()
            v(dve.reciprocal(inv_sqrt_deg1[:, :], small[:, 5, 0:J]))
            e, pe_, cr = small[:, 0, 0:J], small[:, 3, 0:J], small[:, 5, 0:J]
            v(dve.tensor_scalar(e, starts[:, 1:J + 1], 1.0, 0.0, ALU.subtract, ALU.max))
            v(dve.tensor_scalar(pe_, e, (T - 1) / 2.0, 1.0 / T, ALU.subtract, ALU.mult))
            magic(pe_)
            v(dve.scalar_tensor_tensor(cr, pe_, float(T), starts[:, 0:J], ALU.mult, ALU.is_gt))
            v(dve.tensor_scalar(pe_, pe_, float(EP), None, ALU.add))
            v(dve.tensor_tensor(pe_, pe_, e, ALU.subtract))
            v(dve.tensor_tensor(pe_, pe_, cr, ALU.mult))
            v(dve.tensor_tensor(e, e, pe_, ALU.add))
            v(dve.tensor_copy(end_i[:, :], e))

            with dve.Fori(0, WG * P // 8) as it:
                for h in range(2):
                    dve.wait_ge(s_amm, it * 2 + (h + 1))
                    for w in range(4):
                        at = bass.ds(it * 8 + h * 4 + w, 1)
                        dve.tensor_scalar(onehot[:, h, w, 0, :], iota16, key_src[:, at], None, ALU.is_equal)
                        last = dve.tensor_scalar(onehot[:, h, w, 1, :], iota16, key_col[:, at], None, ALU.is_equal)
                    last.then_inc(s_onehot, 1)

            dve.wait_ge(s_amm, 2 + WG * P // 4)
            split(G[:, :, :], scale(G[:, :, :], H[:, :, :], inv_sqrt_deg))
            hop(0)
            v(dve.scalar_tensor_tensor(X[:, :, :], G[:, :, :], -1.0, per_node(inv_sqrt_deg[:, :]), ALU.mult, ALU.mult))
            split(G[:, :, :], scale(G[:, :, :], X[:, :, :], inv_sqrt_deg))
            hop(1)
            v(dve.scalar_tensor_tensor(G[:, :, :], G[:, :, :], -2.0, per_node(inv_sqrt_deg[:, :]), ALU.mult, ALU.mult))
            v(dve.tensor_tensor(G[:, :, :], G[:, :, :], H[:, :, :], ALU.subtract))
            dense(0, dve.memset(XT[D:D + 1, :, :, :], 1.0),
                  lambda ps, at: dve.tensor_scalar(rows(X, at), ps, 0.0, None, ALU.max))
            dve.wait_ge(s_x, 64)
            v(dve.tensor_tensor(X[:, :, :], X[:, :, :], G[:, :, :], ALU.add))

            layernorm(G[:, :, :])
            dense(1, dve.memset(XT[D:D + 1, :, :, :], 1.0), lambda ps, at: dve.tensor_copy(rows(G, at), ps))
            dve.wait_ge(s_y, 32)
            edges(0)
            v(leaky(H[:, :, :]))
            dense(2, dve.memset(XT[D:D + 1, :, :, :], 1.0), lambda ps, at: dve.tensor_copy(rows(G, at), ps))
            dve.wait_ge(s_y, 64)
            edges(1)
            v(leaky(G[:, :, :]))
            v(dve.tensor_tensor(X[:, :, :], X[:, :, :], G[:, :, :], ALU.add))

            layernorm(G[:, :, :])
            for k in (2, 3):
                split(G[:, :, :], scale(G[:, :, :], H[:, :, :], inv_sqrt_deg1))
                hop(k)
                v(scale(H[:, :, :], H[:, :, :], inv_deg1))
                v(scale(G[:, :, :], G[:, :, :], inv_sqrt_deg1))
                v(dve.tensor_tensor(H[:, :, :], H[:, :, :], G[:, :, :], ALU.add))
            v(dve.tensor_tensor(X[:, :, :], X[:, :, :], H[:, :, :], ALU.add))

            layernorm(G[:, :, :])
            split(H[:, :, :], dve.memset(stat[:, 1, :], 0.0))
            hop(4)
            v(scale(G[:, :, :], G[:, :, :], inv_deg))
            dense(3, dve.memset(XT[D:D + 1, :, :, :], 1.0),
                  lambda ps, at: dve.tensor_scalar(rows(H, at), ps, 0.0, None, ALU.max))
            split(H[:, :, :], dve.memset(stat[:, 1, :], 0.0))
            hop(5)
            v(scale(G[:, :, :], G[:, :, :], inv_deg))
            dense(4, dve.memset(XT[D:D + 1, :, :, :], 1.0),
                  lambda ps, at: dve.tensor_tensor(rows(X, at), ps, rows(X, at), ALU.add))


_INS = ['x', 'src', 'dst', 'edge_attr_32', 'L0_gnn_W', 'L0_gnn_b', 'L1_gnn_W1_msg', 'L1_gnn_W1_edge',
        'L1_gnn_W1_root', 'L1_gnn_b1', 'L1_gnn_W2_msg', 'L1_gnn_W2_edge', 'L1_gnn_W2_root', 'L1_gnn_b2',
        'L3_gnn_W_self1', 'L3_gnn_W_neigh1', 'L3_gnn_b1', 'L3_gnn_W_self2', 'L3_gnn_W_neigh2', 'L3_gnn_b2']


def kernel(**inputs):
    import numpy as _np
    import concourse.bacc as _bacc
    from concourse import mybir as _mybir
    from concourse.bass_utils import run_bass_kernel_spmd as _run

    nc = _bacc.Bacc("TRN2", target_bir_lowering=False, num_devices=1)
    arrays, args = {}, []
    for name in _INS:
        a = _np.ascontiguousarray(inputs[name])
        arrays[f"in_{name}"] = a
        args.append(nc.dram_tensor(f"in_{name}", a.shape, _mybir.dt.from_np(a.dtype), kind="ExternalInput").ap())
    out = nc.dram_tensor("out_x", (N, D), F32, kind="ExternalOutput").ap()
    gnn_kernel(nc, *args, out)
    r = _run(nc, [arrays], core_ids=[0])
    return r.results[0]["out_x"]
```

```python
from contextlib import ExitStack

import concourse.bass as bass
from concourse import mybir

ALU = mybir.AluOpType
ACT = mybir.ActivationFunctionType
AX = mybir.AxisListType
F32 = mybir.dt.float32
F16 = mybir.dt.float16
I32 = mybir.dt.int32

P = 128
N = 3125
J = 25
PN = N // J
D = 96
DE = 32
E = 53125
T = 416
EP = P * T
WN = 5
WG = J // WN
WC = WN * J
AC = P * J * J
CH = 16
NCH = T // CH
Q = 4
NQ = CH // Q
HALF = CH // 2
BIG = 3.0e38
MAGIC = 12582912.0
PAIR = 4096.0
PAIR_TOP = 32768.0
GR = 5
NG = J // GR
FIRST = WG + 1
EPS = 1e-5
NO_DST = 4000
NO_KEY = 60000.0


def gnn_kernel(nc, x, src, dst, ea, w0, b0, w1m, w1e, w1r, b1, w2m, w2e, w2r, b2,
               ws1, wn1, b31, ws2, wn2, b32, out):
    ctx = ExitStack()
    with ctx:
        def sb(name, shape, dt):
            return ctx.enter_context(nc.sbuf_tensor(name, shape, dt))

        def sem(name):
            return ctx.enter_context(nc.semaphore(name))

        dst_rows = nc.dram_tensor("dst_rows", [P, T], F32, kind="Internal").ap()
        keys_d = nc.dram_tensor("keys_d", [EP + P, 2], F32, kind="Internal").ap()
        ea_d = nc.dram_tensor("ea_d", [EP, DE], F32, kind="Internal").ap()
        y_d = [nc.dram_tensor(f"y_d{n}", [P * J, D], F32, kind="Internal").ap() for n in range(2)]
        run_d = [nc.dram_tensor(f"run_d{n}", [EP + P, D], F32, kind="Internal").ap() for n in range(2)]

        A = sb("A", [P, AC], F16)
        X = sb("X", [P, J, D], F32)
        H = sb("H", [P, J, D], F32)
        G = sb("G", [P, J, D], F32)
        HL = sb("HL", [P, J, 2 * D], F16)
        XT = sb("XT", [D + 1, 3, 2, P], F32)
        src_i = sb("src_i", [P, T + CH], I32)
        reset = sb("reset", [P, T], F32)
        ident = sb("ident", [P, P], F32)
        carry_reset = sb("carry_reset", [P, P], F32)
        wdense = sb("wdense", [D + 1, 4, D], F32)
        wedge = sb("wedge", [D + 1, 2, 2 * D], F32)
        wattr = sb("wattr", [P, Q * D], F32)
        starts = sb("starts", [P, J + 1], F32)
        inv_deg1 = sb("inv_deg1", [P, J], F32)
        inv_deg = sb("inv_deg", [P, J], F32)
        has_edges = sb("has_edges", [P, J], F32)
        factor = sb("factor", [P, 6, J], F32)
        end_i = sb("end_i", [P, J], I32)
        first_end_i = sb("first_end_i", [P, 1], I32)
        stat = sb("stat", [P, 3, J], F32)
        small = sb("small", [P, 4, J + 1], F32)
        top = sb("top", [P, NG + 3], F32)
        idx_ring = sb("idx_ring", [P, CH], I32)
        row_i = sb("row_i", [P, J + 1], I32)
        win_i = sb("win_i", [P, WG], I32)

        A32 = A[:, :].bitcast(F32)
        used = [0]

        def over_A(columns):
            used[0] += columns
            return A32[:, used[0] - columns:used[0]]

        found_rows = over_A((J + 1) * T).rearrange("p (j t) -> p j t", j=J + 1)
        first_less = over_A((J + 1) * P).rearrange("p (j t) -> p j t", j=J + 1)
        window_keys = over_A(WG * 2 * P).rearrange("p (g e k) -> p g e k", g=WG, k=2)
        row_trash = over_A(T)
        src_f = over_A(T)
        src_hi = over_A(T)
        node_id = over_A(J + 1)
        part_edge = over_A(1)
        no_key = over_A(2)
        window_base = over_A(WG * P)
        ones = over_A(P)
        diag = over_A(2 * P).rearrange("p (a b) -> p a b", a=2)
        zero_rows = over_A(D)
        key_col = over_A(WG * P)
        square0 = over_A(J * D).rearrange("p (j d) -> p j d", d=D)
        G32 = G[:, :, :].rearrange("p j d -> p (j d)")
        HL32 = HL[:, :, :].rearrange("p j d -> p (j d)").bitcast(F32)
        dst_f = G32[:, 0:T]
        dst_i = G32[:, T:2 * T].bitcast(I32)
        keys = G32[:, 2 * T:4 * T].rearrange("p (t k) -> p t k", k=2)
        spread = G32[:, 0:8 * P].bitcast(F16).rearrange("p (h w c) -> p h w c", h=2, w=8)
        iota16 = G32[:, 4 * T:4 * T + P // 2].bitcast(F16)
        o = 4 * T + P // 2
        key16 = G32[:, o:o + WG * P + 16].bitcast(F16).rearrange("p (k w) -> p k w", k=2)
        onehot = HL32[:, 0:16 * P].bitcast(F16).rearrange("p (k h w c) -> p k h w c", k=2, h=2, w=8)
        gathered = HL32[:, 0:CH * D].rearrange("p (t d) -> p t d", d=D)
        o = CH * D
        attr = HL32[:, o:o + CH * DE].rearrange("p (h c) -> p h c", h=2)
        o += CH * DE
        attr_T = HL32[:, o:o + 2 * P].rearrange("p (h c) -> p h c", h=2)
        running = G32[:, 0:CH * D].rearrange("p (t d) -> p t d", d=D)
        o = CH * D
        carry_scan = G32[0:D, o:o + P + 1]
        o += P + 1
        first_seg = G32[:, o:o + D]
        o += D
        crossing = G32[:, o:o + D]
        agg = HL32.rearrange("p (j d) -> p j d", d=D)
        ones_row = carry_reset[0:1, :]

        PSALL = ctx.enter_context(nc.psum_tensor("psall", [P, 8, 512], F32))
        PS = [PSALL[:, n, :] for n in range(8)]

        s_const = sem("const_ready")
        s_pad = sem("edge_pads_set")
        s_padx = sem("node_pads_set")
        s_padw = sem("weight_pads_set")
        s_src = sem("src_loaded")
        s_dst = sem("dst_loaded")
        s_x = sem("x_loaded")
        s_ea0 = sem("zero_rows_set")
        s_ea = sem("edge_attr_copied")
        s_eap = sem("edge_attr_pad_stored")
        s_w0 = sem("dense_weights_loaded")
        s_w02 = sem("weights_combined")
        s_w1 = sem("edge_weights_loaded")
        s_wattr = sem("edge_attr_weights_loaded")
        s_w3 = sem("last_weights_loaded")
        s_dstf = sem("dst_f_ready")
        s_keys = sem("keys_ready")
        s_rows_d = sem("dst_rows_stored")
        s_keys_d = sem("keys_stored")
        s_diag = sem("diag_ready")
        s_bcast = sem("bounds_broadcast")
        s_row_i = sem("row_index_ready")
        s_found = [sem("rows_found_window"), sem("rows_found_rest")]
        s_win_i = sem("window_index_ready")
        s_win = sem("window_keys_found")
        s_winT = sem("window_keys_transposed")
        s_key16 = sem("window_keys_ready")
        s_spread = sem("keys_spread")
        s_onehot = sem("onehot_ready")
        s_amm = sem("adjacency_multiplied")
        s_aev = sem("adjacency_written")
        s_v = sem("vector_steps")
        s_a_in = sem("scalar_input")
        s_a_out = sem("scalar_output")
        s_u = sem("hop_source_ready")
        s_high = sem("high_halves_ready")
        s_split = sem("hop_operand_ready")
        s_hmm = sem("hop_multiplied")
        s_hsum = sem("hop_block_summed")
        s_din = sem("dense_input_ready")
        s_dT = sem("dense_transposed")
        s_dTc = sem("dense_transposed_copied")
        s_dmm = sem("dense_multiplied")
        s_dep = sem("dense_block_done")
        s_root = sem("root_copied")
        s_top = sem("top_ready")
        s_topT = sem("top_transposed")
        s_y = sem("y_stored")
        s_idx = sem("gather_index_ready")
        s_turn = sem("gather_turns")
        s_gat = [sem(f"gathered{q}") for q in range(NQ)]
        s_attr = [sem(f"attr_loaded{h}") for h in range(2)]
        s_aT = sem("attr_transposed")
        s_aTc = sem("attr_transposed_copied")
        s_msg = sem("messages_ready")
        s_scan = sem("scanned")
        s_run = [sem(f"running_stored{h}") for h in range(2)]
        s_lastT = sem("last_state_transposed")
        s_carry = sem("carry_scanned")
        s_carryT = sem("carry_transposed")
        s_fs = sem("first_segment_found")
        s_cross = sem("crossing_ready")
        s_cross_d = sem("crossing_stored")
        s_agg = [sem(f"aggregates_found{g}") for g in range(NG)]
        s_xout = sem("output_ready")
        s_out = sem("out_stored")

        block = ctx.enter_context(nc.Block())

        DENSE = [(2, D), (1, D), (1, 2 * D), (1, 2 * D), (2, D), (2, D)]

        def turned(k, b):
            return PS[5 + (J * k + b) % 3][0:D, 0:DENSE[k][0] * P]

        def product(k, b, a, z):
            return PS[5 + (J * k + b) % 3][:, 2 * P + a:2 * P + z]

        def group(t, g):
            return t[:, g * GR:(g + 1) * GR, :]

        @block.sync
        def _(sp):
            full = (P - 1) * T
            sp.wait_ge(s_pad, 2)
            for edge, tile, done in ((dst, dst_i, s_dst), (src, src_i, s_src)):
                for a, b in ((0, 112), (112, P - 1)):
                    sp.dma_start(tile[a:b, 0:T], edge[a * T:b * T].rearrange("(p t) -> p t", t=T)).then_inc(done, 16)
                sp.dma_start(tile[P - 1:P, 0:E - full], edge[full:E].rearrange("(p t) -> p t", p=1)).then_inc(done, 16)
            sp.wait_ge(s_dstf, 1)
            sp.dma_start(dst_rows, dst_f).then_inc(s_rows_d, 16)
            sp.wait_ge(s_padx, 1)
            for a, b in ((0, 112), (112, PN)):
                sp.dma_start(X[a:b, :, :], x[a * J:b * J, :].rearrange("(p j) d -> p j d", j=J)).then_inc(s_x, 16)
            sp.wait_ge(s_keys, 1)
            sp.dma_start(keys_d[0:EP, :].rearrange("(p t) k -> p t k", t=T), keys).then_inc(s_keys_d, 16)
            sp.dma_start(keys_d[EP:EP + P, :], no_key).then_inc(s_keys_d, 16)
            sp.wait_ge(s_padw, 1)
            sp.dma_start(wdense[0:D, 0:3, :], w0.rearrange("(k d) n -> d k n", d=D)).then_inc(s_w0, 16)
            sp.dma_start(wdense[D:D + 1, 0, :], b0.rearrange("(a n) -> a n", a=1)).then_inc(s_w0, 16)
            for n, (wm, wr, b) in enumerate(((w1m, w1r, b1), (w2m, w2r, b2))):
                sp.dma_start(wedge[0:D, n, 0:D], wm).then_inc(s_w1, 16)
                sp.dma_start(wedge[0:D, n, D:2 * D], wr).then_inc(s_w1, 16)
                sp.dma_start(wedge[D:D + 1, n, D:2 * D], b.rearrange("(a n) -> a n", a=1)).then_inc(s_w1, 16)
            for q in range(Q):
                sp.dma_start(wattr[q * DE:(q + 1) * DE, q * D:(q + 1) * D], w1e).then_inc(s_wattr, 16)
            sp.wait_ge(s_ea0, 1)
            sp.dma_start(ea_d[E:EP, :], zero_rows[0:EP - E, 0:DE]).then_inc(s_eap, 16)
            for n in range(2):
                sp.dma_start(run_d[n][EP:EP + P, :], zero_rows).then_inc(s_run[n], 16)
            sp.wait_ge(s_found[1], 16 * (J + 1 - FIRST))
            sp.dma_start(ea_d[0:E, :].rearrange("(a b c) d -> a b (c d)", a=25, b=17),
                         ea.rearrange("(a b c) d -> a b (c d)", a=25, b=17)).then_inc(s_ea, 16)

            ea_t = ea_d.rearrange("(p t) d -> p (t d)", t=T)
            for n in range(2):
                for g in range(NG):
                    sp.wait_ge(s_dep, J * (n + 2) + (g + 1) * GR)
                    sp.dma_start(y_d[n].rearrange("(p j) d -> p j d", j=J)[:, g * GR:(g + 1) * GR, :],
                                 group(G, g)).then_inc(s_y, 16)
                if n == 0:
                    sp.wait_ge(s_ea, 16)
                    sp.wait_ge(s_eap, 16)
                run_t = run_d[n][0:EP, :].rearrange("(p t) d -> p (t d)", t=T)
                hw = HALF * DE
                sp.wait_ge(s_dep, J * (n + 3))
                for h in range(2):
                    sp.dma_start(attr[:, h, :], ea_t[:, h * hw:(h + 1) * hw]).then_inc(s_attr[h], 16)

                def store(it, h):
                    sp.wait_ge(s_scan, it * CH + (CH + n * T + (h + 1) * HALF))
                    sp.dma_start(run_t[:, bass.ds(it * (CH * D) + h * HALF * D, HALF * D)],
                                 running[:, h * HALF:(h + 1) * HALF, :].rearrange("p t d -> p (t d)")
                                 ).then_inc(s_run[h], 16)

                with sp.Fori(0, NCH - 1) as it:
                    for h in range(2):
                        sp.wait_ge(s_aT, it * NQ + (n * NCH * NQ + 2 * (h + 1)))
                        sp.dma_start(attr[:, h, :], ea_t[:, bass.ds(it * (CH * DE) + CH * DE + h * hw, hw)]
                                     ).then_inc(s_attr[h], 16)
                        store(it, h)
                for h in range(2):
                    store(NCH - 1, h)
                if n == 0:
                    sp.wait_ge(s_msg, 2 + NCH * NQ)
                    for q in range(Q):
                        sp.dma_start(wattr[q * DE:(q + 1) * DE, q * D:(q + 1) * D], w2e).then_inc(s_wattr, 16)
                    for m, w in enumerate((ws1, wn1, ws2, wn2)):
                        sp.dma_start(wdense[0:D, m, :], w).then_inc(s_w3, 16)
                    for m, b in ((0, b31), (2, b32)):
                        sp.dma_start(wdense[D:D + 1, m, :], b.rearrange("(a n) -> a n", a=1)).then_inc(s_w3, 16)
                sp.wait_ge(s_cross, n + 1)
                sp.dma_start(run_d[n][EP:EP + P, :], crossing).then_inc(s_cross_d, 16)
            for g in range(NG):
                sp.wait_ge(s_dep, J * 5 + (g + 1) * GR)
                for a, b in ((0, 112), (112, PN)):
                    sp.dma_start(out[a * J:b * J, :].rearrange("(p j) d -> p j d", j=J)[:, g * GR:(g + 1) * GR, :],
                                 group(X, g)[a:b]).then_inc(s_out, 16)
            sp.wait_ge(s_out, 32 * NG)

        @block.gpsimd
        def _(pool):
            pool.memset(dst_i, NO_DST).then_inc(s_pad, 1)
            pool.memset(src_i[:, :], 0).then_inc(s_pad, 1)
            pool.memset(ident[:, :], 0.0).then_inc(s_const, 1)
            pool.memset(ones, 1.0)
            pool.memset(no_key, NO_KEY)
            pool.wait_ge(s_const, 1)
            pool.affine_select(out=ident[:, :], in_=ident[:, :], compare_op=ALU.not_equal, fill=1.0, base=0,
                               pattern=[[-1, P]], channel_multiplier=1).then_inc(s_const, 1)
            pool.iota(node_id, [[1, J + 1]], base=0, channel_multiplier=J, allow_small_or_imprecise_dtypes=True)
            pool.iota(part_edge, [[0, 1]], base=0, channel_multiplier=T, allow_small_or_imprecise_dtypes=True)
            pool.iota(window_base, [[WC, WG], [J * J, P]], base=0, channel_multiplier=0,
                      allow_small_or_imprecise_dtypes=True)
            pool.iota(iota16, [[1, P]], base=0, channel_multiplier=0,
                      allow_small_or_imprecise_dtypes=True).then_inc(s_const, 1)
            pool.memset(wdense[:, :, :], 0.0)
            pool.memset(wedge[:, :, :], 0.0)
            pool.memset(XT[:, :, :, :], 1.0)
            pool.memset(wattr[:, :], 0.0).then_inc(s_padw, 1)
            pool.memset(zero_rows, 0.0).then_inc(s_ea0, 1)

            def gather(dest, table, index):
                return pool.indirect_dma_start(out=dest, out_offset=None, in_=table,
                                               in_offset=bass.IndirectOffsetOnAxis(ap=index, axis=0))

            pool.wait_ge(s_row_i, 1)
            pool.wait_ge(s_rows_d, 16)
            first = list(range(0, J + 1, WN))
            for j in first:
                gather(found_rows[:, j, :], dst_rows, row_i[:, j:j + 1]).then_inc(s_found[0], 16)
            pool.wait_ge(s_win_i, 1)
            pool.wait_ge(s_keys_d, 32)
            for g in range(WG):
                gather(window_keys[:, g, :, :].rearrange("p e k -> p (e k)"), keys_d,
                       win_i[:, g:g + 1]).then_inc(s_win, 16)
            pool.wait_ge(s_row_i, 2)
            for j in range(J + 1):
                if j not in first:
                    gather(found_rows[:, j, :], dst_rows, row_i[:, j:j + 1]).then_inc(s_found[1], 16)

            for n in range(2):
                pool.wait_ge(s_y, 16 * NG * (n + 1))
                with pool.Fori(0, NCH) as it:
                    for q in range(NQ):
                        pool.wait_ge(s_idx, it * NQ + (n * (NCH + 1) * NQ + q + 1))
                        pool.sem_inc(s_turn, 1)
                        for t in range(q * Q, (q + 1) * Q):
                            gather(gathered[:, t, :], y_d[n], idx_ring[:, t:t + 1]).then_inc(s_gat[q], 16)
                for h in range(2):
                    pool.wait_ge(s_run[h], 16 * (NCH * (n + 1) + 1))
                gather(first_seg, run_d[n], first_end_i[:, 0:1]).then_inc(s_fs, 16)
                pool.wait_ge(s_cross_d, 16 * (n + 1))
                for j in range(J):
                    gather(agg[:, j, :], run_d[n], end_i[:, j:j + 1]).then_inc(s_agg[j // GR], 16)

        @block.tensor
        def _(pe):
            pe.wait_ge(s_const, 2)
            pe.wait_ge(s_diag, 1)
            for m in range(2):
                mm = pe.matmul(PS[7][:, m * P:(m + 1) * P], ones, diag[:, m, :], start=True, stop=True)
            mm.then_inc(s_bcast, 1)
            pe.wait_ge(s_win, 16 * WG)
            for m in range(2 * WG):
                k, g = divmod(m, WG)
                mm = pe.transpose(PS[m // 4][:, (m % 4) * P:(m % 4 + 1) * P], window_keys[:, g, :, k], ident[:, :])
            mm.then_inc(s_winT, 1)
            with pe.Fori(0, WG * P // 16) as it:
                for h in range(2):
                    pe.wait_ge(s_onehot, it * 2 + (h + 1))
                    pe.wait_ge(s_aev, it * 2 + (h + 1))
                    for w in range(8):
                        mm = pe.matmul(PS[4 + 2 * h + w // 4][:, (w % 4) * WC:(w % 4 + 1) * WC],
                                       onehot[:, 0, h, w, :], onehot[:, 1, h, w, 0:WC], start=True, stop=True)
                    mm.then_inc(s_amm, 1)

            by_slot = A[:, :].rearrange("p (n b j) -> p n b j", b=J, j=J)

            def hop(k):
                for b in range(J):
                    pe.wait_ge(s_hsum, J * k + b + 1)
                    for j in range(J):
                        if b == 0 and j % GR == 0:
                            pe.wait_ge(s_split, NG * k + j // GR + 1)
                        mm = pe.matmul(PS[b % 5][:, 0:2 * D], by_slot[:, :, b, j], HL[:, j, :],
                                       start=(j == 0), stop=(j == J - 1))
                    mm.then_inc(s_hmm, 1)

            def dense(k, inputs, weights, biased=True):
                m, w = DENSE[k]

                def turn(b):
                    if b % GR == 0:
                        pe.wait_ge(s_din, NG * k + b // GR + 1)
                    if J * k + b >= 3:
                        pe.wait_ge(s_dep, J * k + b - 2)
                    for i, blocks in enumerate(inputs):
                        tr = pe.transpose(turned(k, b)[:, i * P:(i + 1) * P], blocks[:, b, :], ident[:, :])
                    tr.then_inc(s_dT, 1)

                turn(0)
                for b in range(J):
                    if b < J - 1:
                        turn(b + 1)
                    pe.wait_ge(s_dTc, J * k + b + 1)
                    for i in range(m):
                        rows = D + 1 if i == 0 and biased else D
                        mm = pe.matmul(product(k, b, 0, w), XT[0:rows, (J * k + b) % 3, i, :], weights[i][0:rows],
                                       start=(i == 0), stop=(i == m - 1))
                    mm.then_inc(s_dmm, 1)

            def edges(n):
                pe.wait_ge(s_wattr, 16 * Q * (n + 1))
                with pe.Fori(0, NCH) as it:
                    def turn(q):
                        if q % 2 == 0:
                            pe.wait_ge(s_attr[q // 2], it * 16 + 16 * (n * NCH + 1))
                        pe.wait_ge(s_aTc, it * NQ + (n * NCH * NQ + q + 1))
                        pe.transpose(PS[4 + q % 2][:, 0:P], attr[:, q // 2, (q % 2) * P:(q % 2 + 1) * P],
                                     ident[:, :]).then_inc(s_aT, 1)

                    turn(0)
                    for q in range(NQ):
                        if q < NQ - 1:
                            turn(q + 1)
                        pe.wait_ge(s_aTc, it * NQ + (n * NCH * NQ + q + 1 + 2))
                        pe.wait_ge(s_scan, it * CH + (n * T + (q + 1) * Q))
                        pe.matmul(PS[q][:, 0:Q * D], attr_T[:, q % 2, :], wattr[:, :], start=True, stop=False)
                        pe.wait_ge(s_gat[q], it * (16 * Q) + 16 * Q * (n * NCH + 1))
                        pe.matmul(PS[q][:, 0:Q * D], ident[:, :],
                                  gathered[:, q * Q:(q + 1) * Q, :].rearrange("p t d -> p (t d)"),
                                  start=False, stop=True).then_inc(s_msg, 1)
                pe.wait_ge(s_scan, CH + (n + 1) * T)
                pe.transpose(PS[6][0:D, 0:P], running[:, CH - 1, :], ident[:, :]).then_inc(s_lastT, 1)
                pe.wait_ge(s_carry, n + 1)
                pe.transpose(PS[7][:, 0:D], carry_scan[:, 0:P], ident[0:D, 0:D]).then_inc(s_carryT, 1)

            pe.wait_ge(s_aev, 2 + WG * P // 8)
            hop(0)
            pe.wait_ge(s_w02, 1)
            pe.wait_ge(s_padw, 1)
            dense(0, (H, G), [wdense[:, 0, :], wdense[:, 1, :]])
            hop(1)
            dense(1, (G,), [wdense[:, 2, :]], biased=False)
            pe.wait_ge(s_w1, 6 * 16)
            dense(2, (H,), [wedge[:, 0, :]])
            edges(0)
            dense(3, (H,), [wedge[:, 1, :]])
            edges(1)
            hop(2)
            hop(3)
            hop(4)
            pe.wait_ge(s_w3, 6 * 16)
            dense(4, (H, G), [wdense[:, 0, :], wdense[:, 1, :]])
            pe.wait_ge(s_top, 1)
            pe.transpose(PS[7][0:1, 0:P], top[:, NG:NG + 1], ident[:, :]).then_inc(s_topT, 1)
            pe.wait_ge(s_top, 2)
            pe.matmul(PS[6][:, 0:2], ones_row, top[0:1, NG:NG + 2], start=True, stop=True).then_inc(s_topT, 1)
            hop(5)
            dense(5, (H, G), [wdense[:, 2, :], wdense[:, 3, :]])

        @block.scalar
        def _(act):
            asked = [0]

            def on_request(out_, in_, func):
                asked[0] += 1
                act.wait_ge(s_a_in, asked[0])
                act.activation(out_, in_, func).then_inc(s_a_out, 1)

            def split(k, source, scale=1.0):
                if k:
                    act.wait_ge(s_hmm, J * k)
                for g in range(NG):
                    act.wait_ge(s_u, NG * max(k - 1, 0) + g + 1)
                    act.activation(group(HL, g)[:, :, 0:D], group(source, g), ACT.Copy, scale=scale
                                   ).then_inc(s_high, 1)

            def root(g):
                on_request(stat[:, 2, g * GR:(g + 1) * GR], stat[:, 1, g * GR:(g + 1) * GR], ACT.Sqrt)

            def dense(k, copied=None, after_group=None):
                m, w = DENSE[k]
                for b in range(J + 1):
                    if b < J:
                        act.wait_ge(s_dT, J * k + b + 1)
                        if J * k + b >= 3:
                            act.wait_ge(s_dmm, J * k + b - 2)
                        act.activation(XT[0:D, (J * k + b) % 3, 0:m, :], turned(k, b).rearrange("p (m c) -> p m c", m=m),
                                       ACT.Copy).then_inc(s_dTc, 1)
                    if copied and b:
                        act.wait_ge(s_dmm, J * k + b)
                        act.activation(H[:, b - 1, :], product(k, b - 1, copied, copied + D) if copied > 0 else
                                       product(k, b - 1, 0, D), ACT.Copy).then_inc(s_root if copied > 0 else s_dep, 1)
                    if after_group and b and b % GR == 0:
                        after_group(b // GR - 1)

            def edges(n):
                def index(q, it):
                    act.activation(idx_ring[:, q * Q:(q + 1) * Q], src_i[:, bass.ds(it * CH + q * Q, Q)],
                                   ACT.Copy).then_inc(s_idx, 1)

                act.wait_ge(s_dep, J * (n + 3))
                for q in range(NQ):
                    index(q, 0)
                with act.Fori(0, NCH) as it:
                    for q in range(NQ):
                        act.wait_ge(s_aT, it * NQ + (n * NCH * NQ + q + 1))
                        act.wait_ge(s_msg, it * NQ + (n * NCH * NQ + q + 1))
                        act.activation(attr_T[:, q % 2, :], PS[4 + q % 2][:, 0:P], ACT.Copy).then_inc(s_aTc, 1)
                        act.wait_ge(s_msg, it * NQ + (n * NCH * NQ + q + 1 + 2))
                        index(q, it + 1)

            for g in range(NG):
                root(g)
            act.wait_ge(s_rows_d, 16)
            act.wait_ge(s_keys_d, 32)
            act.wait_ge(s_eap, 16)
            for h in range(2):
                act.wait_ge(s_run[h], 16)
            act.wait_ge(s_key16, 1)

            def spread_keys(at, h):
                act.activation(spread[:, h, :, :], key16[:, 0, at].unsqueeze(2).to_broadcast([P, 8, P]),
                               ACT.Copy).then_inc(s_spread, 1)

            for h in range(2):
                spread_keys(slice(h * 8, h * 8 + 8), h)
            windows = A[:, :].rearrange("p (w c) -> p w c", c=J * J)
            with act.Fori(0, WG) as g:
                with act.Fori(0, P // 16) as i:
                    for h in range(2):
                        act.wait_ge(s_amm, g * (P // 8) + i * 2 + (2 + h + 1))
                        act.activation(
                            windows[:, bass.ds(i * 16 + h * 8, 8), bass.ds(g * WC, WC)].rearrange(
                                "p (a w) c -> p a w c", a=2),
                            PSALL[:, 4 + 2 * h:6 + 2 * h, 0:4 * WC].rearrange("p a (w c) -> p a w c", w=4),
                            ACT.Copy).then_inc(s_aev, 1)
                        spread_keys(bass.ds(g * P + i * 16 + (16 + h * 8), 8), h)
            on_request(small[:, 3, 0:J], small[:, 2, 0:J], ACT.Sqrt)
            on_request(factor[:, 5, :], factor[:, 4, :], ACT.Sqrt)
            split(0, G)
            dense(0, copied=-1)
            dense(1, after_group=root)
            dense(2, copied=D)
            edges(0)
            dense(3, copied=D)
            edges(1)
            for g in range(NG):
                root(g)
            split(2, G)
            split(3, G)
            for g in range(NG):
                root(g)
            split(4, H, PAIR)
            dense(4)
            split(5, H, top[:, NG + 2:NG + 3])
            dense(5)

        @block.vector
        def _(dve):
            steps = [0]
            asks = [0]

            def v(instruction):
                steps[0] += 1
                instruction.then_inc(s_v, 1)
                dve.wait_ge(s_v, steps[0])

            def ask(instruction):
                asks[0] += 1
                instruction.then_inc(s_a_in, 1)
                dve.wait_ge(s_a_out, asks[0])

            def per_node(t, n=GR):
                return t.unsqueeze(2).to_broadcast([P, n, D])

            def of(t, g):
                return t[:, g * GR:(g + 1) * GR]

            def scale(out_, in_, by, g):
                return dve.tensor_tensor(out_, in_, per_node(of(by, g)), ALU.mult)

            def to_integer(t):
                v(dve.tensor_scalar(t, t, MAGIC, MAGIC, ALU.add, ALU.subtract))

            def layernorm(g, square, last_in=None):
                xg, hg = group(X, g), group(H, g)
                s0, s1, s2 = (of(stat[:, i, :], g) for i in range(3))
                v(dve.tensor_reduce(s0, xg, AX.X, ALU.add))
                v(dve.scalar_tensor_tensor(hg, per_node(s0), -1.0 / D, xg, ALU.mult, ALU.add))
                v(dve.tensor_tensor(square, hg, hg, ALU.mult))
                v(dve.tensor_reduce(s1, square, AX.X, ALU.add))
                ask(dve.tensor_scalar(s1, s1, 1.0 / D, EPS, ALU.mult, ALU.add))
                v(dve.reciprocal(s0, s2))
                return dve.scalar_tensor_tensor(hg, hg, 0.0, per_node(s0), ALU.max, ALU.mult)

            def split(k, source, by=1.0):
                for g in range(NG):
                    dve.wait_ge(s_high, NG * max(k - 1, 0) + g + 1)
                    dve.scalar_tensor_tensor(group(HL, g)[:, :, D:2 * D], group(source, g), by,
                                             group(HL, g)[:, :, 0:D], ALU.mult, ALU.subtract).then_inc(s_split, 1)

            def hop(k, finish):
                for g in range(NG):
                    for b in range(g * GR, (g + 1) * GR):
                        dve.wait_ge(s_hmm, J * k + b + 1)
                        dve.tensor_reduce(G[:, b, :], PS[b % 5][:, 0:2 * D].rearrange("p (k d) -> p d k", k=2),
                                          AX.X, ALU.add).then_inc(s_hsum, 1)
                    dve.wait_ge(s_hsum, 5 + J * k + (g + 1) * GR)
                    finish(g)

            def dense(k, block_step, finish=None):
                m, w = DENSE[k]
                for g in range(NG):
                    for b in range(g * GR, (g + 1) * GR):
                        dve.wait_ge(s_dmm, J * k + b + 1)
                        if w > D:
                            dve.wait_ge(s_root, J * (k - 2) + b + 1)
                        block_step(b).then_inc(s_dep, 1)
                    dve.wait_ge(s_dep, J * k + (g + 1) * GR)
                    if finish:
                        finish(g)

            def edges(n, finish):
                v(dve.memset(running[:, CH - 1, :], -BIG))
                v(dve.memset(carry_scan[:, 0:1], -BIG))
                with dve.Fori(0, NCH) as it:
                    for q in range(NQ):
                        dve.wait_ge(s_msg, it * NQ + (n * NCH * NQ + q + 1 + 2))
                        if q % 2 == 0:
                            dve.wait_ge(s_run[q // 2], it * 16 + 16 * (n * NCH + 1))
                        for i in range(Q):
                            t = q * Q + i
                            dve.wait_ge(s_scan, it * CH + (CH + n * T + t))
                            dve.scalar_tensor_tensor(running[:, t, :], running[:, (t - 1) % CH, :],
                                                     reset[:, bass.ds(it * CH + t, 1)],
                                                     PS[q][:, i * D:(i + 1) * D], ALU.add, ALU.max
                                                     ).then_inc(s_scan, 1)
                dve.wait_ge(s_lastT, n + 1)
                dve.tensor_tensor_scan(carry_scan[:, 1:P + 1], carry_reset[0:D, :], PS[6][0:D, 0:P], -BIG,
                                       ALU.add, ALU.max).then_inc(s_carry, 1)
                dve.wait_ge(s_carryT, n + 1)
                dve.wait_ge(s_fs, 16 * (n + 1))
                dve.tensor_tensor(crossing, PS[7][:, 0:D], first_seg, ALU.max).then_inc(s_cross, 1)
                for g in range(NG):
                    dve.wait_ge(s_agg[g], 16 * GR * (n + 1))
                    v(scale(group(agg, g), group(agg, g), has_edges, g))
                    v(dve.tensor_tensor(group(agg, g), group(agg, g), group(H, g), ALU.add))
                    finish(g)

            def leaky(out_, g):
                return dve.scalar_tensor_tensor(out_, group(agg, g), 0.01, group(agg, g), ALU.mult, ALU.max)

            for signal, count in ((s_aev, 2), (s_hsum, 5), (s_scan, CH), (s_aTc, 2), (s_msg, 2), (s_amm, 2)):
                dve.sem_inc(signal, count)
            dve.memset(X[:, :, :], 0.0).then_inc(s_padx, 1)

            dve.wait_ge(s_dst, 48)
            dve.tensor_copy(dst_f, dst_i).then_inc(s_dstf, 1)
            dve.wait_ge(s_const, 3)
            dve.wait_ge(s_dstf, 1)
            dve.tensor_scalar(diag[:, 0, :], ident[:, :], dst_f[:, 0:1], None, ALU.mult)
            dve.tensor_scalar(diag[:, 1, :], ident[:, :], dst_f[:, T - 1:T], None, ALU.mult).then_inc(s_diag, 1)
            dve.wait_ge(s_src, 48)
            v(dve.tensor_copy(src_f, src_i[:, 0:T]))
            dve.wait_ge(s_bcast, 1)
            firsts = PS[7][:, 0:P]
            row = small[:, 0, :]
            v(dve.tensor_tensor(first_less[:, 0:FIRST, :], firsts.unsqueeze(1).to_broadcast([P, FIRST, P]),
                                node_id[:, 0:J + 1:WN].unsqueeze(2).to_broadcast([P, FIRST, P]), ALU.is_lt))
            v(dve.tensor_reduce(row[:, 0:J + 1:WN], first_less[:, 0:FIRST, :], AX.X, ALU.add))
            v(dve.tensor_scalar(row[:, 0:J + 1:WN], row[:, 0:J + 1:WN], 1.0, 0.0, ALU.subtract, ALU.max))
            dve.tensor_copy(row_i[:, 0:J + 1:WN], row[:, 0:J + 1:WN]).then_inc(s_row_i, 1)
            v(dve.tensor_scalar(src_hi, src_f, 1.0 / J, 0.48, ALU.mult, ALU.subtract))
            to_integer(src_hi)
            v(dve.scalar_tensor_tensor(src_f, src_hi, -float(J), src_f, ALU.mult, ALU.add))
            v(dve.tensor_copy(keys[:, :, 0], src_hi))
            dve.scalar_tensor_tensor(keys[:, :, 1], dst_f, float(J), src_f, ALU.mult, ALU.add).then_inc(s_keys, 1)

            def inner(t):
                return t[:, 0:J].rearrange("p (a r) -> p a r", r=WN)[:, :, 1:WN]

            some = first_less[:, 0:WG * (WN - 1), :].rearrange("p (a r) c -> p a r c", a=WG)
            v(dve.tensor_tensor(some, firsts.unsqueeze(1).unsqueeze(1).to_broadcast([P, WG, WN - 1, P]),
                                inner(node_id).unsqueeze(3).to_broadcast([P, WG, WN - 1, P]), ALU.is_lt))
            v(dve.tensor_reduce(inner(row), some, AX.X, ALU.add))
            v(dve.tensor_scalar(inner(row), inner(row), 1.0, 0.0, ALU.subtract, ALU.max))
            dve.tensor_copy(inner(row_i[:, :]), inner(row)).then_inc(s_row_i, 1)

            def count(j):
                v(dve.tensor_scalar(row_trash, found_rows[:, j, :], node_id[:, j:j + 1], None, ALU.is_lt, ALU.add,
                                    accum_out=small[:, 1, j:j + 1]))

            dve.wait_ge(s_found[0], 16 * FIRST)
            for j in range(0, J + 1, WN):
                count(j)
            at = slice(0, J + 1, WN)
            v(dve.scalar_tensor_tensor(starts[:, at], row[:, at], float(T), small[:, 1, at], ALU.mult, ALU.add))
            dve.tensor_copy(win_i[:, :], starts[:, 0:J:WN]).then_inc(s_win_i, 1)

            v(dve.memset(reset[:, 0:1], 0.0))
            v(dve.tensor_tensor(reset[:, 1:T], dst_f[:, 1:T], dst_f[:, 0:T - 1], ALU.not_equal))
            v(dve.tensor_scalar(reset[:, :], reset[:, :], -BIG, None, ALU.mult))
            v(dve.memset(carry_reset[:, 0:1], -BIG))
            v(dve.tensor_copy(diag[:, 1, :], PS[7][:, P:2 * P]))
            v(dve.tensor_tensor(carry_reset[:, 1:P], diag[:, 1, 1:P], diag[:, 1, 0:P - 1], ALU.not_equal))
            v(dve.tensor_scalar(carry_reset[:, 1:P], carry_reset[:, 1:P], -BIG, None, ALU.mult))
            one = small[:, 2, 0:1]
            v(dve.tensor_scalar(row_trash, dst_f, dst_f[:, 0:1], None, ALU.is_equal, ALU.add, accum_out=one))
            v(dve.scalar_tensor_tensor(one, one, -1.0, part_edge, ALU.add, ALU.add))
            v(dve.tensor_copy(first_end_i[:, :], one))

            dve.wait_ge(s_x, 32)
            for g in range(NG):
                v(layernorm(g, group(square0, g)))

            dve.wait_ge(s_winT, 1)
            v(dve.memset(key16[:, :, :], 0.0))
            flat = PSALL[:, 0:3, :].rearrange("p a c -> p (a c)")
            v(dve.tensor_copy(key16[:, 0, 0:WG * P], flat[:, 0:WG * P]))
            v(dve.tensor_tensor(key_col, flat[:, WG * P:2 * WG * P], window_base, ALU.subtract))
            dve.tensor_scalar(key16[:, 1, 0:WG * P], key_col, -1.0, float(P - 1), ALU.max, ALU.min
                              ).then_inc(s_key16, 1)
            dve.wait_ge(s_found[1], 16 * (J + 1 - FIRST))
            for j in range(J + 1):
                if j % WN:
                    count(j)
            at = slice(0, J + 1)
            v(dve.scalar_tensor_tensor(starts[:, at], row[:, at], float(T), small[:, 1, at], ALU.mult, ALU.add))

            e, last, crosses = small[:, 1, 0:J], small[:, 2, 0:J], small[:, 3, 0:J]
            v(dve.tensor_scalar(e, starts[:, 1:J + 1], 1.0, 0.0, ALU.subtract, ALU.max))
            v(dve.tensor_scalar(last, e, (T - 1) / 2.0, 1.0 / T, ALU.subtract, ALU.mult))
            to_integer(last)
            v(dve.scalar_tensor_tensor(crosses, last, float(T), starts[:, 0:J], ALU.mult, ALU.is_gt))
            v(dve.tensor_scalar(last, last, float(EP), None, ALU.add))
            v(dve.tensor_tensor(last, last, e, ALU.subtract))
            v(dve.tensor_tensor(last, last, crosses, ALU.mult))
            v(dve.tensor_tensor(e, e, last, ALU.add))
            v(dve.tensor_copy(end_i[:, :], e))

            dve.wait_ge(s_key16, 1)
            with dve.Fori(0, WG * P // 16) as it:
                for h in range(2):
                    dve.wait_ge(s_amm, it * 2 + (h + 1))
                    dve.tensor_tensor(
                        onehot[:, 1, h, :, 0:WC], iota16[:, 0:WC].unsqueeze(1).to_broadcast([P, 8, WC]),
                        key16[:, 1, bass.ds(it * 16 + h * 8, 8)].unsqueeze(2).to_broadcast([P, 8, WC]),
                        ALU.is_equal)
                    dve.wait_ge(s_spread, it * 2 + (h + 1))
                    dve.tensor_tensor(onehot[:, 0, h, :, :], iota16.unsqueeze(1).to_broadcast([P, 8, P]),
                                      spread[:, h, :, :], ALU.is_equal).then_inc(s_onehot, 1)

            deg = small[:, 1, 0:J]
            v(dve.tensor_tensor(deg, starts[:, 1:J + 1], starts[:, 0:J], ALU.subtract))
            v(dve.tensor_scalar(has_edges[:, :], deg, 1.0, None, ALU.min))
            v(dve.tensor_scalar(factor[:, 4, :], deg, 1.0, None, ALU.add))
            v(dve.reciprocal(inv_deg1[:, :], factor[:, 4, :]))
            ask(dve.tensor_scalar(small[:, 2, 0:J], deg, 1.0, None, ALU.max))
            ask(dve.reciprocal(inv_deg[:, :], small[:, 2, 0:J]))
            v(dve.reciprocal(small[:, 1, 0:J], small[:, 3, 0:J]))
            v(dve.reciprocal(small[:, 2, 0:J], factor[:, 5, :]))
            inv_sqrt, inv_sqrt1 = small[:, 1, 0:J], small[:, 2, 0:J]
            for i, (t, by) in enumerate(((inv_sqrt, PAIR), (inv_sqrt, -1.0 / PAIR), (inv_sqrt, -2.0 / PAIR),
                                         (inv_sqrt1, PAIR), (inv_sqrt1, 1.0 / PAIR), (inv_deg[:, :], 1.0 / PAIR))):
                v(dve.tensor_scalar(factor[:, i, :], t, by, None, ALU.mult))

            dve.wait_ge(s_w0, 32)
            dve.tensor_tensor(wdense[0:D, 0, :], wdense[0:D, 0, :], wdense[0:D, 2, :], ALU.subtract
                              ).then_inc(s_w02, 1)
            dve.wait_ge(s_amm, 2 + WG * P // 8)
            dve.wait_ge(s_spread, WG * P // 8 + 2)
            for g in range(NG):
                scale(group(G, g), group(H, g), factor[:, 0, :], g).then_inc(s_u, 1)
            split(0, G)

            def cheb1(g):
                scale(group(G, g), group(G, g), factor[:, 1, :], g).then_inc(s_din, 1)

            hop(0, cheb1)
            for g in range(NG):
                dve.wait_ge(s_din, g + 1)
                v(scale(group(HL, g)[:, :, 0:D], group(G, g), factor[:, 0, :], g))
                for j in range(g * GR, (g + 1) * GR):
                    low = dve.scalar_tensor_tensor(HL[:, j, D:2 * D], G[:, j, :], factor[:, 0, j:j + 1],
                                                   HL[:, j, 0:D], ALU.mult, ALU.subtract)
                low.then_inc(s_split, 1)

            def cheb2(g):
                scale(group(G, g), group(G, g), factor[:, 2, :], g).then_inc(s_din, 1)

            hop(1, cheb2)

            def layer1_in(g):
                v(dve.scalar_tensor_tensor(group(X, g), group(H, g), 0.0, group(X, g), ALU.max, ALU.add))
                layernorm(g, group(G, g)).then_inc(s_din, 1)

            dense(1, lambda b: dve.tensor_tensor(H[:, b, :], product(1, b, 0, D), H[:, b, :], ALU.add), layer1_in)

            dense(2, lambda b: dve.tensor_copy(G[:, b, :], product(2, b, 0, D)))
            dve.wait_ge(s_y, 16 * NG)
            edges(0, lambda g: leaky(group(H, g), g).then_inc(s_din, 1))
            dense(3, lambda b: dve.tensor_copy(G[:, b, :], product(3, b, 0, D)))
            dve.wait_ge(s_y, 32 * NG)

            def layer2_in(g):
                v(leaky(group(G, g), g))
                v(dve.tensor_tensor(group(X, g), group(X, g), group(G, g), ALU.add))
                v(layernorm(g, group(G, g)))
                scale(group(G, g), group(H, g), factor[:, 3, :], g).then_inc(s_u, 1)

            edges(1, layer2_in)

            def looped(g):
                v(scale(group(H, g), group(H, g), inv_deg1, g))
                v(scale(group(G, g), group(G, g), factor[:, 4, :], g))
                v(dve.tensor_tensor(group(H, g), group(H, g), group(G, g), ALU.add))

            def hop2_out(g):
                looped(g)
                scale(group(G, g), group(H, g), factor[:, 3, :], g).then_inc(s_u, 1)

            def hop3_out(g):
                looped(g)
                v(dve.tensor_tensor(group(X, g), group(X, g), group(H, g), ALU.add))
                layernorm(g, group(G, g)).then_inc(s_u, 1)

            split(2, G)
            hop(2, hop2_out)
            split(3, G)
            hop(3, hop3_out)

            split(4, H, PAIR)
            hop(4, lambda g: scale(group(G, g), group(G, g), factor[:, 5, :], g).then_inc(s_din, 1))
            dense(4, lambda b: dve.tensor_scalar(H[:, b, :], product(4, b, 0, D), 0.0, None, ALU.max),
                  lambda g: v(dve.tensor_reduce(top[:, g:g + 1], group(H, g), AX.XY, ALU.max)))
            v(dve.memset(ones_row, 1.0))
            dve.tensor_reduce(top[:, NG:NG + 1], top[:, 0:NG], AX.X, ALU.max).then_inc(s_top, 1)
            dve.wait_ge(s_topT, 1)
            v(dve.tensor_reduce(top[0:1, 0:1], PS[7][0:1, 0:P], AX.X, ALU.max))
            v(dve.tensor_scalar(top[0:1, NG:NG + 1], top[0:1, 0:1], 1e-20, 1.0 / PAIR_TOP, ALU.max, ALU.mult))
            dve.reciprocal(top[0:1, NG + 1:NG + 2], top[0:1, NG:NG + 1]).then_inc(s_top, 1)
            dve.wait_ge(s_topT, 2)
            v(dve.tensor_copy(top[:, NG + 1:NG + 3], PS[6][:, 0:2]))
            dve.tensor_scalar(factor[:, 5, :], inv_deg[:, :], top[:, NG + 1:NG + 2], None, ALU.mult
                              ).then_inc(s_u, NG)
            split(5, H, top[:, NG + 2:NG + 3])
            hop(5, lambda g: scale(group(G, g), group(G, g), factor[:, 5, :], g).then_inc(s_din, 1))
            dense(5, lambda b: dve.tensor_tensor(X[:, b, :], product(5, b, 0, D), X[:, b, :], ALU.add))


_INS = ['x', 'src', 'dst', 'edge_attr_32', 'L0_gnn_W', 'L0_gnn_b', 'L1_gnn_W1_msg', 'L1_gnn_W1_edge',
        'L1_gnn_W1_root', 'L1_gnn_b1', 'L1_gnn_W2_msg', 'L1_gnn_W2_edge', 'L1_gnn_W2_root', 'L1_gnn_b2',
        'L3_gnn_W_self1', 'L3_gnn_W_neigh1', 'L3_gnn_b1', 'L3_gnn_W_self2', 'L3_gnn_W_neigh2', 'L3_gnn_b2']


def kernel(**inputs):
    import numpy as _np
    import concourse.bacc as _bacc
    from concourse import mybir as _mybir
    from concourse.bass_utils import run_bass_kernel_spmd as _run

    nc = _bacc.Bacc("TRN2", target_bir_lowering=False, num_devices=1)
    arrays, args = {}, []
    for name in _INS:
        a = _np.ascontiguousarray(inputs[name])
        arrays[f"in_{name}"] = a
        args.append(nc.dram_tensor(f"in_{name}", a.shape, _mybir.dt.from_np(a.dtype), kind="ExternalInput").ap())
    out = nc.dram_tensor("out_x", (N, D), F32, kind="ExternalOutput").ap()
    gnn_kernel(nc, *args, out)
    r = _run(nc, [arrays], core_ids=[0])
    return r.results[0]["out_x"]
```

```python
from contextlib import ExitStack

import concourse.bass as bass
from concourse import mybir

ALU = mybir.AluOpType
ACT = mybir.ActivationFunctionType
AX = mybir.AxisListType
F32 = mybir.dt.float32
F16 = mybir.dt.float16
I32 = mybir.dt.int32

P = 128
N = 3125
J = 25
PN = N // J
D = 96
DE = 32
E = 53125
T = 416
EP = P * T
WN = 5
WG = J // WN
WC = WN * J
AC = P * J * J
CH = 16
NCH = T // CH
Q = 4
NQ = CH // Q
HALF = CH // 2
PICKS = 3
SUMMED = 2
PICKED = CH - PICKS
LENT = 9600
BIG = 3.0e38
MAGIC = 1.5 * 2.0 ** 23
PAIR = 4096.0
PAIR_TOP = 32768.0
GR = 5
NG = J // GR
FIRST = WG + 1
HALVES = P // 8
STEPS = -(-GR * J // (HALVES - 2))
EPS = 1e-5
ZERO_ROW = float(EP + P)
NO_DST = 4000
NO_KEY = 60000.0


def gnn_kernel(nc, x, src, dst, ea, w0, b0, w1m, w1e, w1r, b1, w2m, w2e, w2r, b2,
               ws1, wn1, b31, ws2, wn2, b32, out):
    ctx = ExitStack()
    with ctx:
        def sb(name, shape, dt):
            return ctx.enter_context(nc.sbuf_tensor(name, shape, dt))

        def sem(name):
            return ctx.enter_context(nc.semaphore(name))

        dst_rows = nc.dram_tensor("dst_rows", [P, T], F32, kind="Internal").ap()
        keys_d = nc.dram_tensor("keys_d", [EP + P, 2], F32, kind="Internal").ap()
        ea_d = nc.dram_tensor("ea_d", [EP, DE], F32, kind="Internal").ap()
        y_d = [nc.dram_tensor(f"y_d{n}", [P * J, D], F32, kind="Internal").ap() for n in range(2)]
        run_d = [nc.dram_tensor(f"run_d{n}", [EP + 2 * P, D], F32, kind="Internal").ap() for n in range(2)]
        lent_d = nc.dram_tensor("lent_d", [P, LENT], F32, kind="Internal").ap()

        A = sb("A", [P, AC], F16)
        X = sb("X", [P, J, D], F32)
        H = sb("H", [P, J, D], F32)
        G = sb("G", [P, J, D], F32)
        HL = sb("HL", [P, J, 2 * D], F16)
        XT = sb("XT", [P, 3, 2, P], F32)
        src_i = sb("src_i", [P, T + CH], I32)
        reset = sb("reset", [P, T], F32)
        ident = sb("ident", [P, P], F32)
        carry_reset = sb("carry_reset", [P, P], F32)
        weights = sb("weights", [P, 3 * 4 * D], F32)
        wdense = weights[0:D + 1, 0:4 * D].rearrange("p (m n) -> p m n", m=4)
        wedge = weights[0:D + 1, 4 * D:8 * D].rearrange("p (m n) -> p m n", m=2)
        wattr = weights[:, 8 * D:12 * D]
        starts = sb("starts", [P, J + 1], F32)
        inv_deg1 = sb("inv_deg1", [P, J], F32)
        inv_deg = sb("inv_deg", [P, J], F32)
        has_edges = sb("has_edges", [P, J], F32)
        factor = sb("factor", [P, 6, J], F32)
        end_i = sb("end_i", [P, J], I32)
        first_end_i = sb("first_end_i", [P, 1], I32)
        stat = sb("stat", [P, 3, J], F32)
        small = sb("small", [P, 4, J + 1], F32)
        top = sb("top", [P, NG + 3], F32)
        idx_ring = sb("idx_ring", [P, CH], I32)
        row_i = sb("row_i", [P, J + 1], I32)
        win_i = sb("win_i", [P, WG], I32)
        rounds_i = sb("rounds_i", [1, 1], I32)

        A32 = A[:, :].bitcast(F32)
        used = [0]

        def over_A(columns):
            used[0] += columns
            return A32[:, used[0] - columns:used[0]]

        found_rows = over_A((J + 1) * T).rearrange("p (j t) -> p j t", j=J + 1)
        first_less = over_A((J + 1) * P).rearrange("p (j t) -> p j t", j=J + 1)
        window_keys = over_A(WG * 2 * P).rearrange("p (g e k) -> p g e k", g=WG, k=2)
        row_trash = over_A(T)
        sign_trash = over_A(T)
        half_off = over_A(J + 1)
        src_f = over_A(T)
        src_hi = over_A(T)
        node_id = over_A(J + 1)
        part_edge = over_A(1)
        no_key = over_A(2)
        window_base = over_A(WG * P)
        ones = over_A(P)
        diag = over_A(2 * P).rearrange("p (a b) -> p a b", a=2)
        zero_rows = over_A(2 * D)
        key_col = over_A(WG * P)
        square0 = over_A(J * D).rearrange("p (j d) -> p j d", d=D)
        G32 = G[:, :, :].rearrange("p j d -> p (j d)")
        HL32 = HL[:, :, :].rearrange("p j d -> p (j d)").bitcast(F32)
        dst_f = G32[:, 0:T]
        dst_i = G32[:, T:2 * T].bitcast(I32)
        keys = G32[:, 2 * T:4 * T].rearrange("p (t k) -> p t k", k=2)
        spread = weights[:, 0:8 * P].bitcast(F16).rearrange("p (h w c) -> p h w c", h=2, w=8)
        XT32 = XT[:, :, :, :].rearrange("p a b c -> p (a b c)")
        iota16 = XT32[:, 0:P // 2].bitcast(F16)
        key16 = XT32[:, P // 2:P // 2 + WG * P + 16].bitcast(F16).rearrange("p (k w) -> p k w", k=2)
        X32 = X[:, :, :].rearrange("p j d -> p (j d)")
        onehot = X32[:, 0:16 * P].bitcast(F16).rearrange("p (k h w c) -> p k h w c", k=2, h=2, w=8)
        more_keys = G32[:, 0:WG * 2 * P].rearrange("p (g e k) -> p g e k", g=WG, k=2)
        first_column = X32[:, 17 * P:18 * P]
        more_col = X32[:, 16 * P:17 * P]
        gathered = HL32[:, 0:CH * D].rearrange("p (t d) -> p t d", d=D)
        o = CH * D
        attr = HL32[:, o:o + CH * DE].rearrange("p (h c) -> p h c", h=2)
        o += CH * DE
        attr_T = HL32[:, o:o + 2 * P].rearrange("p (h c) -> p h c", h=2)
        running = G32[:, 0:CH * D].rearrange("p (t d) -> p t d", d=D)
        o = CH * D
        carry_scan = G32[0:D, o:o + P + 1]
        o += P + 1
        first_seg = G32[:, o:o + D]
        o += D
        crossing = G32[:, o:o + D]
        lent = A32[:, AC // 2 - LENT:AC // 2]
        lent_used = [0]

        def lent_columns(columns):
            lent_used[0] += columns
            return lent[:, lent_used[0] - columns:lent_used[0]]

        parts = lent_columns(J * 2 * D // 2).bitcast(F16).rearrange("p (j k d) -> p j k d", k=2, d=D)
        pick = lent_columns(PICKS * J * P // 2).bitcast(F16).rearrange("p (a j e) -> p a j e", a=PICKS, j=J)
        slot_id = lent_columns(J * P // 2).bitcast(F16).rearrange("p (j e) -> p j e", j=J)
        own_slot = lent_columns(PICKS * P // 2).bitcast(F16)
        src_diag = lent_columns(PICKS * P)
        all_ones = lent_columns(P)
        src_column = lent_columns(PICKS)
        first_node = lent_columns(1)
        table_scale, table_unscale = top[:, NG + 2:NG + 3], top[:, NG + 1:NG + 2]
        agg = HL32.rearrange("p (j d) -> p j d", d=D)
        ones_row = carry_reset[0:1, :]

        PSALL = ctx.enter_context(nc.psum_tensor("psall", [P, 8, 512], F32))
        PS = [PSALL[:, n, :] for n in range(8)]

        s_const = sem("const_ready")
        s_pad = sem("edge_pads_set")
        s_padx = sem("node_pads_set")
        s_padw = sem("weight_pads_set")
        s_src = sem("src_loaded")
        s_dst = sem("dst_loaded")
        s_x = sem("x_loaded")
        s_ea0 = sem("zero_rows_set")
        s_ea = sem("edge_attr_copied")
        s_eap = sem("edge_attr_pad_stored")
        s_w0 = sem("dense_weights_loaded")
        s_w02 = sem("weights_combined")
        s_w1 = sem("edge_weights_loaded")
        s_wattr = sem("edge_attr_weights_loaded")
        s_w3 = sem("last_weights_loaded")
        s_dstf = sem("dst_f_ready")
        s_keys = sem("keys_ready")
        s_rows_d = sem("dst_rows_stored")
        s_keys_d = sem("keys_stored")
        s_diag = sem("diag_ready")
        s_bcast = sem("bounds_broadcast")
        s_row_i = sem("row_index_ready")
        s_found = [sem("rows_found_windows")] + [sem(f"rows_found_rest{a}") for a in range(WG)]
        s_half = sem("count_offsets_ready")
        s_counted = sem("starts_counted")
        s_win_i = sem("window_index_ready")
        s_win = sem("window_keys_found")
        s_winT = sem("window_keys_transposed")
        s_key16 = sem("window_keys_ready")
        s_spread = sem("keys_spread")
        s_onehot = sem("onehot_ready")
        s_amm = sem("adjacency_multiplied")
        s_aev = sem("adjacency_written")
        s_built = sem("adjacency_built")
        s_padT = sem("ones_row_set")
        s_more_hmm = sem("repeated_hop_multiplied")
        s_more_sum = sem("repeated_hop_summed")
        s_rounds = sem("further_rounds_counted")
        s_more_v = sem("further_vector_steps")
        s_more_turn = sem("further_turns")
        s_more_win = sem("further_window_index_ready")
        s_more_keys = sem("further_keys_found")
        s_more_T = sem("further_keys_transposed")
        s_more_onehot = sem("further_onehot_ready")
        s_more_mm = sem("further_adjacency_multiplied")
        s_more_add = sem("further_adjacency_added")
        s_v = sem("vector_steps")
        s_a_in = sem("scalar_input")
        s_a_out = sem("scalar_output")
        s_u = sem("hop_source_ready")
        s_high = sem("high_halves_ready")
        s_split = sem("hop_operand_ready")
        s_hmm = sem("hop_multiplied")
        s_hsum = sem("hop_block_summed")
        s_din = sem("dense_input_ready")
        s_dT = sem("dense_transposed")
        s_dTc = sem("dense_transposed_copied")
        s_dmm = sem("dense_multiplied")
        s_dep = sem("dense_block_done")
        s_root = sem("root_copied")
        s_top = sem("top_ready")
        s_topT = sem("top_transposed")
        s_y = sem("y_stored")
        s_idx = sem("gather_index_ready")
        s_turn = sem("gather_turns")
        s_gat = [sem(f"gathered{q}") for q in range(NQ)]
        s_attr = [sem(f"attr_loaded{h}") for h in range(2)]
        s_aT = sem("attr_transposed")
        s_aTc = sem("attr_transposed_copied")
        s_msg = sem("messages_ready")
        s_scan = sem("scanned")
        s_run = [sem(f"running_stored{h}") for h in range(2)]
        s_lastT = sem("last_state_transposed")
        s_carry = sem("carry_scanned")
        s_carryT = sem("carry_transposed")
        s_fs = sem("first_segment_found")
        s_lent = sem("lent_space_stored")
        s_back = sem("lent_space_restored")
        s_pickc = sem("pick_constants_ready")
        s_scale = sem("table_scale_steps")
        s_scaleT = sem("table_scale_spread")
        s_part1 = sem("table_high_halves_ready")
        s_parts = sem("parts_ready")
        s_srcc = sem("source_column_ready")
        s_srcd = sem("source_diagonal_ready")
        s_srcb = sem("source_broadcast")
        s_own = sem("own_slots_ready")
        s_pick = sem("pick_ready")
        s_pmm = sem("picked_multiplied")
        s_picked = sem("picked_column_ready")
        s_message = sem("messages_added")
        s_cross = sem("crossing_ready")
        s_cross_d = sem("crossing_stored")
        s_agg = [sem(f"aggregates_found{g}") for g in range(NG)]
        s_out = sem("out_stored")

        block = ctx.enter_context(nc.Block())

        DENSE = [(2, D), (1, D), (1, 2 * D), (1, 2 * D), (2, D), (2, D)]

        dense_order = [(0, g) for g in range(NG)]
        for r in range(NG + 2):
            dense_order += [(k, r - k) for k in (1, 2) if 0 <= r - k < NG]
        dense_order += [(k, g) for k in (3, 4, 5) for g in range(NG)]
        input_order = [(0, g) for g in range(NG)]
        for r in range(NG + 1):
            input_order += [(k, r + 1 - k) for k in (1, 2) if 0 <= r + 1 - k < NG]
        input_order += [(k, g) for k in (3, 4, 5) for g in range(NG)]

        def at(k, b):
            return dense_order.index((k, b // GR)) * GR + b % GR

        def group_done(k, g):
            return at(k, (g + 1) * GR - 1) + 1

        def turned(k, b):
            return PS[5 + at(k, b) % 3][0:D, 0:DENSE[k][0] * P]

        def product(k, b, a, z):
            return PS[5 + at(k, b) % 3][:, 2 * P + a:2 * P + z]

        def blocks_of(*groups):
            return [(k, b) for k, g in groups for b in range(g * GR, (g + 1) * GR)]

        def round_groups(r):
            return [(k, r - k) for k in (1, 2) if 0 <= r - k < NG]

        def group(t, g):
            return t[:, g * GR:(g + 1) * GR, :]

        @block.sync
        def _(sp):
            full = (P - 1) * T
            sp.wait_ge(s_pad, 2)
            for edge, tile, done in ((dst, dst_i, s_dst), (src, src_i, s_src)):
                for a, b in ((0, 112), (112, P - 1)):
                    sp.dma_start(tile[a:b, 0:T], edge[a * T:b * T].rearrange("(p t) -> p t", t=T)).then_inc(done, 16)
                sp.dma_start(tile[P - 1:P, 0:E - full], edge[full:E].rearrange("(p t) -> p t", p=1)).then_inc(done, 16)
            sp.wait_ge(s_dstf, 1)
            sp.dma_start(dst_rows, dst_f).then_inc(s_rows_d, 16)
            sp.wait_ge(s_padx, 1)
            for a, b in ((0, 112), (112, PN)):
                sp.dma_start(X[a:b, :, :], x[a * J:b * J, :].rearrange("(p j) d -> p j d", j=J)).then_inc(s_x, 16)
            sp.wait_ge(s_keys, 1)
            sp.dma_start(keys_d[0:EP, :].rearrange("(p t) k -> p t k", t=T), keys).then_inc(s_keys_d, 16)
            sp.dma_start(keys_d[EP:EP + P, :], no_key).then_inc(s_keys_d, 16)
            sp.wait_ge(s_ea0, 1)
            sp.dma_start(ea_d[E:EP, :], zero_rows[0:EP - E, 0:DE]).then_inc(s_eap, 16)
            for n in range(2):
                sp.dma_start(run_d[n][EP:EP + 2 * P, :].rearrange("(p a) d -> p (a d)", a=2), zero_rows
                             ).then_inc(s_run[n], 16)
            sp.wait_ge(s_found[WG], 16 * (WN - 1))
            sp.dma_start(ea_d[0:E, :].rearrange("(a b c) d -> a b (c d)", a=25, b=17),
                         ea.rearrange("(a b c) d -> a b (c d)", a=25, b=17)).then_inc(s_ea, 16)
            sp.wait_ge(s_padw, 1)
            sp.dma_start(wdense[0:D, 0:3, :], w0.rearrange("(k d) n -> d k n", d=D)).then_inc(s_w0, 16)
            sp.dma_start(wdense[D:D + 1, 0, :], b0.rearrange("(a n) -> a n", a=1)).then_inc(s_w0, 16)
            for n, (wm, wr, b) in enumerate(((w1m, w1r, b1), (w2m, w2r, b2))):
                sp.dma_start(wedge[0:D, n, 0:D], wm).then_inc(s_w1, 16)
                sp.dma_start(wedge[0:D, n, D:2 * D], wr).then_inc(s_w1, 16)
                sp.dma_start(wedge[D:D + 1, n, D:2 * D], b.rearrange("(a n) -> a n", a=1)).then_inc(s_w1, 16)
            for q in range(Q):
                sp.dma_start(wattr[q * DE:(q + 1) * DE, q * D:(q + 1) * D], w1e).then_inc(s_wattr, 16)
            sp.wait_ge(s_padx, 2)
            for a, b in ((0, 112), (112, PN)):
                sp.dma_start(X[a:b, :, :], x[a * J:b * J, :].rearrange("(p j) d -> p j d", j=J)).then_inc(s_x, 16)

            sp.dma_start(lent_d, lent).then_inc(s_lent, 16)

            ea_t = ea_d.rearrange("(p t) d -> p (t d)", t=T)
            for n in range(2):
                for g in range(NG):
                    sp.wait_ge(s_dep, group_done(n + 2, g))
                    sp.dma_start(y_d[n].rearrange("(p j) d -> p j d", j=J)[:, g * GR:(g + 1) * GR, :],
                                 group(G, g)).then_inc(s_y, 16)
                if n == 0:
                    sp.wait_ge(s_ea, 16)
                    sp.wait_ge(s_eap, 16)
                run_t = run_d[n][0:EP, :].rearrange("(p t) d -> p (t d)", t=T)
                hw = HALF * DE
                sp.wait_ge(s_dep, group_done(n + 2, NG - 1))
                for h in range(2):
                    sp.dma_start(attr[:, h, :], ea_t[:, h * hw:(h + 1) * hw]).then_inc(s_attr[h], 16)

                def store(it, h):
                    sp.wait_ge(s_scan, it * CH + (CH + n * T + (h + 1) * HALF))
                    sp.dma_start(run_t[:, bass.ds(it * (CH * D) + h * HALF * D, HALF * D)],
                                 running[:, h * HALF:(h + 1) * HALF, :].rearrange("p t d -> p (t d)")
                                 ).then_inc(s_run[h], 16)

                with sp.Fori(0, NCH - 1) as it:
                    for h in range(2):
                        sp.wait_ge(s_aT, it * NQ + (n * NCH * NQ + 2 * (h + 1)))
                        sp.dma_start(attr[:, h, :], ea_t[:, bass.ds(it * (CH * DE) + CH * DE + h * hw, hw)]
                                     ).then_inc(s_attr[h], 16)
                        store(it, h)
                for h in range(2):
                    store(NCH - 1, h)
                if n == 0:
                    sp.wait_ge(s_msg, 2 + NCH * NQ)
                    for q in range(Q):
                        sp.dma_start(wattr[q * DE:(q + 1) * DE, q * D:(q + 1) * D], w2e).then_inc(s_wattr, 16)
                    for m, w in enumerate((ws1, wn1, ws2, wn2)):
                        sp.dma_start(wdense[0:D, m, :], w).then_inc(s_w3, 16)
                    for m, b in ((0, b31), (2, b32)):
                        sp.dma_start(wdense[D:D + 1, m, :], b.rearrange("(a n) -> a n", a=1)).then_inc(s_w3, 16)
                sp.wait_ge(s_cross, n + 1)
                sp.dma_start(run_d[n][EP:EP + P, :], crossing).then_inc(s_cross_d, 16)
            for g in range(NG):
                if g:
                    sp.wait_ge(s_agg[g - 1], 16 * GR * 2)
                piece = slice(g * LENT // NG, (g + 1) * LENT // NG)
                sp.dma_start(lent[:, piece], lent_d[:, piece]).then_inc(s_back, 16)
            for g in range(NG):
                sp.wait_ge(s_dep, group_done(5, g))
                for a, b in ((0, 112), (112, PN)):
                    sp.dma_start(out[a * J:b * J, :].rearrange("(p j) d -> p j d", j=J)[:, g * GR:(g + 1) * GR, :],
                                 group(X, g)[a:b]).then_inc(s_out, 16)
            sp.wait_ge(s_out, 32 * NG)

        @block.gpsimd
        def _(pool):
            pool.memset(dst_i, NO_DST).then_inc(s_pad, 1)
            pool.memset(src_i[:, :], 0).then_inc(s_pad, 1)
            pool.memset(ident[:, :], 0.0).then_inc(s_const, 1)
            pool.memset(ones, 1.0)
            pool.memset(no_key, NO_KEY)
            pool.wait_ge(s_const, 1)
            pool.affine_select(out=ident[:, :], in_=ident[:, :], compare_op=ALU.not_equal, fill=1.0, base=0,
                               pattern=[[-1, P]], channel_multiplier=1).then_inc(s_const, 1)
            pool.iota(node_id, [[1, J + 1]], base=0, channel_multiplier=J, allow_small_or_imprecise_dtypes=True)
            pool.iota(part_edge, [[0, 1]], base=0, channel_multiplier=T, allow_small_or_imprecise_dtypes=True)
            pool.iota(window_base, [[WC, WG], [J * J, P]], base=0, channel_multiplier=0,
                      allow_small_or_imprecise_dtypes=True)
            pool.iota(iota16, [[1, P]], base=0, channel_multiplier=0,
                      allow_small_or_imprecise_dtypes=True).then_inc(s_const, 1)
            pool.memset(zero_rows, 0.0).then_inc(s_ea0, 1)

            def gather(dest, table, index):
                return pool.indirect_dma_start(out=dest, out_offset=None, in_=table,
                                               in_offset=bass.IndirectOffsetOnAxis(ap=index, axis=0))

            pool.wait_ge(s_row_i, 1)
            pool.wait_ge(s_rows_d, 16)
            first = list(range(0, J + 1, WN))
            for j in first:
                gather(found_rows[:, j, :], dst_rows, row_i[:, j:j + 1]).then_inc(s_found[0], 16)
            pool.wait_ge(s_win_i, 1)
            pool.wait_ge(s_keys_d, 32)
            for g in range(WG):
                gather(window_keys[:, g, :, :].rearrange("p e k -> p (e k)"), keys_d,
                       win_i[:, g:g + 1]).then_inc(s_win, 16)
            pool.wait_ge(s_row_i, 2)
            for j in range(J + 1):
                if j not in first:
                    gather(found_rows[:, j, :], dst_rows, row_i[:, j:j + 1]).then_inc(s_found[1 + j // WN], 16)
            pool.wait_ge(s_amm, 2 + WG * P // 8)
            pool.wait_ge(s_spread, WG * P // 8 + 2)
            pool.memset(weights[:, :], 0.0).then_inc(s_padw, 1)
            pool.wait_ge(s_rounds, 1)
            rounds = pool.value_load(rounds_i[0:1, 0:1], min_val=0, max_val=T)
            with pool.If(rounds):
                pool.iota(first_column, [[J * J, P]], base=0, channel_multiplier=0,
                          allow_small_or_imprecise_dtypes=True).then_inc(s_more_v, 1)
            with pool.If(rounds), pool.Fori(0, rounds) as r:
                pool.wait_ge(s_more_win, r + 1)
                pool.sem_inc(s_turn, 1)
                for g in range(WG):
                    gather(more_keys[:, g, :, :].rearrange("p e k -> p (e k)"), keys_d,
                           win_i[:, g:g + 1]).then_inc(s_more_keys, 16)
            pool.wait_ge(s_built, 1)
            pool.memset(XT[:, :, :, :], 1.0).then_inc(s_padT, 1)
            pool.memset(X[:, :, :], 0.0).then_inc(s_padx, 1)

            pool.wait_ge(s_lent, 16)
            pool.wait_ge(s_hmm, 2 * J)
            pool.iota(slot_id, [[1, J], [0, P]], base=0, channel_multiplier=0, allow_small_or_imprecise_dtypes=True)
            pool.iota(first_node, [[0, 1]], base=0, channel_multiplier=-J, allow_small_or_imprecise_dtypes=True)
            pool.memset(all_ones, 1.0).then_inc(s_pickc, 1)

            for n in range(2):
                pool.wait_ge(s_y, 16 * NG * (n + 1))
                with pool.Fori(0, NCH) as it:
                    for q in range(NQ):
                        pool.wait_ge(s_idx, it * NQ + (n * (NCH * NQ + NQ - 2) + q + 1))
                        pool.sem_inc(s_turn, 1)
                        for t in range(q * Q, min((q + 1) * Q, PICKED)):
                            gather(gathered[:, t, :], y_d[n], idx_ring[:, t:t + 1]).then_inc(s_gat[q], 16)
                for h in range(2):
                    pool.wait_ge(s_run[h], 16 * (NCH * (n + 1) + 1))
                gather(first_seg, run_d[n], first_end_i[:, 0:1]).then_inc(s_fs, 16)
                pool.wait_ge(s_cross_d, 16 * (n + 1))
                for j in range(J):
                    gather(agg[:, j, :], run_d[n], end_i[:, j:j + 1]).then_inc(s_agg[j // GR], 16)

        @block.tensor
        def _(pe):
            pe.wait_ge(s_const, 2)
            pe.wait_ge(s_diag, 1)
            for m in range(2):
                mm = pe.matmul(PS[7][:, m * P:(m + 1) * P], ones, diag[:, m, :], start=True, stop=True)
            mm.then_inc(s_bcast, 1)
            def turn_keys(found):
                for m in range(2 * WG):
                    k, g = divmod(m, WG)
                    mm = pe.transpose(PS[m // 4][:, (m % 4) * P:(m % 4 + 1) * P], found[:, g, :, k], ident[:, :])
                return mm

            pe.wait_ge(s_win_i, 1)
            pe.transpose(PS[3][0:1, 0:P], top[:, 0:1], ident[:, :])
            pe.wait_ge(s_win, 16 * WG)
            turn_keys(window_keys).then_inc(s_winT, 1)
            by_slot = A[:, :].rearrange("p (n b j) -> p n b j", b=J, j=J)

            def first_hop(b, j):
                if j == 0:
                    pe.wait_ge(s_hsum, b + 2)
                if b == 0 and j % GR == 0:
                    pe.wait_ge(s_split, j // GR + 1)
                mm = pe.matmul(PS[b % 4][:, 0:2 * D], by_slot[:, :, b, j], HL[:, j, :],
                               start=(j == 0), stop=(j == J - 1))
                if j == J - 1:
                    mm.then_inc(s_hmm, 1)

            def build(half):
                pe.wait_ge(s_onehot, half + 1)
                pe.wait_ge(s_aev, half + 1)
                h = half % 2
                for w in range(8):
                    mm = pe.matmul(PS[4 + 2 * h + w // 4][:, (w % 4) * WC:(w % 4 + 1) * WC],
                                   onehot[:, 0, h, w, :], onehot[:, 1, h, w, 0:WC], start=True, stop=True)
                mm.then_inc(s_amm, 1)

            for g in range(WG + 1):
                todo = [(b, j) for b in range((g - 1) * GR, g * GR) for j in range(J)] if g else []
                for half in range(HALVES if g < WG else 0):
                    build(g * HALVES + half)
                    if half == 2 and g:
                        pe.wait_ge(s_aev, 2 + HALVES * g)
                    for b, j in todo[:STEPS] if half >= 2 else []:
                        first_hop(b, j)
                    if half >= 2:
                        todo = todo[STEPS:]
                if g == WG:
                    pe.wait_ge(s_aev, 2 + HALVES * WG)
                for b, j in todo:
                    first_hop(b, j)

            pe.wait_ge(s_rounds, 1)
            rounds = pe.value_load(rounds_i[0:1, 0:1], min_val=0, max_val=T)
            with pe.If(rounds), pe.Fori(0, rounds) as r:
                pe.wait_ge(s_more_keys, r * (16 * WG) + 16 * WG)
                turn_keys(more_keys).then_inc(s_more_T, 1)
                with pe.Fori(0, WG * P // 8) as i:
                    pe.wait_ge(s_more_onehot, r * (WG * P // 8) + i + 1)
                    for w in range(8):
                        mm = pe.matmul(PS[4 + w // 4][:, (w % 4) * WC:(w % 4 + 1) * WC],
                                       onehot[:, 0, 0, w, :], onehot[:, 1, 0, w, 0:WC], start=True, stop=True)
                    mm.then_inc(s_more_mm, 1)
                pe.wait_ge(s_more_add, r * (WG * P // 8) + WG * P // 8)
            with pe.If(rounds), pe.Fori(0, J) as b:
                pe.wait_ge(s_more_sum, b + 1)
                for j in range(J):
                    mm = pe.matmul(PS[0][:, 0:2 * D], A[:, bass.ds(b * J + j, P, step=J * J)], HL[:, j, :],
                                   start=(j == 0), stop=(j == J - 1))
                mm.then_inc(s_more_hmm, 1)

            def hop(k, g):
                group_blocks = range(g * GR, (g + 1) * GR)
                if g == 0:
                    todo = [(b, j) for jg in range(NG) for b in group_blocks for j in range(jg * GR, (jg + 1) * GR)]
                else:
                    todo = [(b, j) for b in group_blocks for j in range(J)]
                for b, j in todo:
                    if b == 0 and j % GR == 0:
                        pe.wait_ge(s_split, NG * k + j // GR + 1)
                    if j == 0:
                        pe.wait_ge(s_hsum, J * k + b + 1)
                    mm = pe.matmul(PS[b % 5][:, 0:2 * D], by_slot[:, :, b, j], HL[:, j, :],
                                   start=(j == 0), stop=(j == J - 1))
                    if j == J - 1:
                        mm.then_inc(s_hmm, 1)

            def dense(blocks, inputs, weights):
                def turn(k, b):
                    n = at(k, b)
                    if b % GR == 0:
                        pe.wait_ge(s_din, input_order.index((k, b // GR)) + 1)
                    if n >= 3:
                        pe.wait_ge(s_dep, n - 2)
                    for i, tile in enumerate(inputs[k]):
                        tr = pe.transpose(turned(k, b)[:, i * P:(i + 1) * P], tile[:, b, :], ident[:, :])
                    tr.then_inc(s_dT, 1)

                turn(*blocks[0])
                for (k, b), following in zip(blocks, blocks[1:] + [None]):
                    if following:
                        turn(*following)
                    n = at(k, b)
                    m, w = DENSE[k]
                    pe.wait_ge(s_dTc, n + 1)
                    for i in range(m):
                        rows = D if i or k == 1 else D + 1
                        mm = pe.matmul(product(k, b, 0, w), XT[0:rows, n % 3, i, :], weights[k][i][0:rows],
                                       start=(i == 0), stop=(i == m - 1))
                    mm.then_inc(s_dmm, 1)

            def edges(n):
                pe.wait_ge(s_wattr, 16 * Q * (n + 1))
                pe.wait_ge(s_pickc, 1)

                def broadcast(count):
                    pe.wait_ge(s_srcd, count)
                    pe.matmul(PS[7][:, 0:PICKS * P], all_ones, src_diag, start=True, stop=True).then_inc(s_srcb, 1)

                pe.wait_ge(s_scale, 3 * n + 1)
                pe.transpose(PS[7][0:1, 0:P], top[:, 0:1], ident[:, :]).then_inc(s_scaleT, 1)
                pe.wait_ge(s_scale, 3 * n + 2)
                pe.matmul(PS[6][:, 0:2], all_ones[0:1, :], top[0:1, NG:NG + 2], start=True, stop=True
                          ).then_inc(s_scaleT, 1)
                broadcast(n * (NCH + 1) + 1)
                pe.wait_ge(s_parts, NG * (n + 1))
                with pe.Fori(0, NCH) as it:
                    def turn(q):
                        if q % 2 == 0:
                            pe.wait_ge(s_attr[q // 2], it * 16 + 16 * (n * NCH + 1))
                        pe.wait_ge(s_aTc, it * NQ + (n * NCH * NQ + q + 1))
                        pe.transpose(PS[4 + q % 2][:, 0:P], attr[:, q // 2, (q % 2) * P:(q % 2 + 1) * P],
                                     ident[:, :]).then_inc(s_aT, 1)

                    turn(0)
                    for q in range(NQ):
                        if q < NQ - 1:
                            turn(q + 1)
                        pe.wait_ge(s_aTc, it * NQ + (n * NCH * NQ + q + 1 + 2))
                        if q < SUMMED:
                            pe.wait_ge(s_scan, it * CH + (n * T + (q + 1) * Q))
                        else:
                            k = NQ - SUMMED
                            pe.wait_ge(s_message, it * k + (n * NCH * k + q - SUMMED + 1))
                        mm = pe.matmul(PS[q][:, 0:Q * D], attr_T[:, q % 2, :], wattr[:, :],
                                       start=True, stop=(q >= SUMMED))
                        if q < SUMMED:
                            pe.wait_ge(s_gat[q], it * (16 * Q) + 16 * Q * (n * NCH + 1))
                            mm = pe.matmul(PS[q][:, 0:Q * D], ident[:, :],
                                           gathered[:, q * Q:(q + 1) * Q, :].rearrange("p t d -> p (t d)"),
                                           start=False, stop=True)
                        mm.then_inc(s_msg, 1)
                        if q < PICKS:
                            pe.wait_ge(s_pick, it * PICKS + (PICKS * n * (NCH + 1) + q + 1))
                            pe.wait_ge(s_picked, it * PICKS + (PICKS * n * NCH + q + 1))
                            for j in range(J):
                                mm = pe.matmul(PS[6][:, 0:2 * D], pick[:, q, j, :],
                                               parts[:, j, :, :].rearrange("p k d -> p (k d)"),
                                               start=(j == 0), stop=(j == J - 1))
                            mm.then_inc(s_pmm, 1)
                        if q == 0:
                            broadcast(it + (n * (NCH + 1) + 2))
                pe.wait_ge(s_own, (n + 1) * (NCH + 1))
                pe.wait_ge(s_scan, CH + (n + 1) * T)
                pe.transpose(PS[6][0:D, 0:P], running[:, CH - 1, :], ident[:, :]).then_inc(s_lastT, 1)
                pe.wait_ge(s_carry, n + 1)
                pe.transpose(PS[7][:, 0:D], carry_scan[:, 0:P], ident[0:D, 0:D]).then_inc(s_carryT, 1)

            inputs = [(H, G), (G,), (H,), (H,), (H, G), (H, G)]
            used = [(wdense[:, 0, :], wdense[:, 1, :]), (wdense[:, 2, :],), (wedge[:, 0, :],), (wedge[:, 1, :],),
                    (wdense[:, 0, :], wdense[:, 1, :]), (wdense[:, 2, :], wdense[:, 3, :])]
            pe.wait_ge(s_w02, 1)
            pe.wait_ge(s_padT, 1)
            dense(blocks_of(*((0, g) for g in range(NG))), inputs, used)
            pe.wait_ge(s_w1, 6 * 16)
            for r in range(NG + 2):
                if r < NG:
                    hop(1, r)
                if r:
                    dense(blocks_of(*round_groups(r)), inputs, used)
            edges(0)
            for g in range(NG):
                dense(blocks_of((3, g)), inputs, used)
            edges(1)
            pe.wait_ge(s_back, 16 * NG)
            for g in range(NG):
                hop(2, g)
            for g in range(NG):
                hop(3, g)
            pe.wait_ge(s_w3, 6 * 16)
            for k in (4, 5):
                if k == 5:
                    pe.wait_ge(s_top, 1)
                    pe.transpose(PS[7][0:1, 0:P], top[:, NG:NG + 1], ident[:, :]).then_inc(s_topT, 1)
                    pe.wait_ge(s_top, 2)
                    pe.matmul(PS[6][:, 0:2], ones_row, top[0:1, NG:NG + 2], start=True, stop=True
                              ).then_inc(s_topT, 1)
                for r in range(NG + 1):
                    if r < NG:
                        hop(k, r)
                    if r:
                        dense(blocks_of((k, r - 1)), inputs, used)

        @block.scalar
        def _(act):
            asked = [0]

            def on_request(out_, in_, func):
                asked[0] += 1
                act.wait_ge(s_a_in, asked[0])
                act.activation(out_, in_, func).then_inc(s_a_out, 1)

            def high(k, g, source, scale=1.0):
                act.wait_ge(s_u, NG * max(k - 1, 0) + g + 1)
                act.activation(group(HL, g)[:, :, 0:D], group(source, g), ACT.Copy, scale=scale
                               ).then_inc(s_high, 1)

            def split(k, source, scale=1.0):
                if k:
                    act.wait_ge(s_hmm, J * k)
                for g in range(NG):
                    high(k, g, source, scale)

            def root(g):
                on_request(stat[:, 2, g * GR:(g + 1) * GR], stat[:, 1, g * GR:(g + 1) * GR], ACT.Sqrt)

            def dense(blocks, roots=False):
                for now, before in zip(blocks + [None], [None] + blocks):
                    if now:
                        n, m = at(*now), DENSE[now[0]][0]
                        act.wait_ge(s_dT, n + 1)
                        if n >= 3:
                            act.wait_ge(s_dmm, n - 2)
                        act.activation(XT[0:D, n % 3, 0:m, :], turned(*now).rearrange("p (m c) -> p m c", m=m),
                                       ACT.Copy).then_inc(s_dTc, 1)
                    if before and before[0] == 0:
                        act.wait_ge(s_dmm, at(*before) + 1)
                        act.activation(H[:, before[1], :], product(*before, 0, D), ACT.Copy).then_inc(s_dep, 1)
                    if before and before[0] in (2, 3):
                        act.wait_ge(s_dmm, at(*before) + 1)
                        act.activation(H[:, before[1], :], product(*before, D, 2 * D), ACT.Copy).then_inc(s_root, 1)

            def edges(n):
                def index(q, it):
                    act.activation(idx_ring[:, q * Q:(q + 1) * Q], src_i[:, bass.ds(it * CH + q * Q, Q)],
                                   ACT.Copy).then_inc(s_idx, 1)

                act.wait_ge(s_dep, group_done(n + 2, NG - 1))
                for q in range(NQ - 2):
                    index(q, 0)
                def diagonals(first, count):
                    act.activation(src_column, src_i[:, first], ACT.Copy).then_inc(s_srcc, 1)
                    act.wait_ge(s_srcc, count)
                    for a in range(PICKS):
                        diagonal = act.activation(src_diag[:, a * P:(a + 1) * P], ident[:, :], ACT.Copy,
                                                  scale=src_column[:, a:a + 1])
                    diagonal.then_inc(s_srcd, 1)

                def own(count, picks):
                    act.wait_ge(s_srcb, count)
                    if picks is not None:
                        act.wait_ge(s_pick, picks)
                    act.activation(own_slot, PS[7][:, 0:PICKS * P], ACT.Identity, bias=first_node
                                   ).then_inc(s_own, 1)

                act.wait_ge(s_pickc, 1)
                diagonals(slice(PICKED, CH), n * (NCH + 1) + 1)
                act.wait_ge(s_scale, 3 * n + 3)
                for g in range(NG):
                    act.activation(group(parts, g)[:, :, 0, :], group(G, g), ACT.Copy, scale=table_scale
                                   ).then_inc(s_part1, 1)
                own(n * (NCH + 1) + 1, PICKS * n * (NCH + 1) if n else None)
                with act.Fori(0, NCH) as it:
                    for q in range(NQ):
                        act.wait_ge(s_aT, it * NQ + (n * NCH * NQ + q + 1))
                        act.wait_ge(s_msg, it * NQ + (n * NCH * NQ + q + 1))
                        act.activation(attr_T[:, q % 2, :], PS[4 + q % 2][:, 0:P], ACT.Copy).then_inc(s_aTc, 1)
                        act.wait_ge(s_scan, it * CH + (n * T + CH + (q - 1) * Q))
                        index((q + 2) % NQ, it if q < 2 else it + 1)
                        if q == 0:
                            diagonals(bass.ds(it * CH + (CH + PICKED), PICKS), it + (n * (NCH + 1) + 2))
                        if q == 1:
                            own(it + (n * (NCH + 1) + 2), it * PICKS + PICKS * (n * (NCH + 1) + 1))

            def count_signs(a):
                act.wait_ge(s_found[1 + a], 16 * (WN - 1))
                for j in range(a * WN + 1, (a + 1) * WN):
                    if j > 1:
                        act.wait_ge(s_counted, j - 1 - a)
                    act.activation(sign_trash, found_rows[:, j, :], ACT.Sign, bias=half_off[:, j:j + 1],
                                   accum_out=small[:, 3, j:j + 1]).then_inc(s_counted, 1)

            root(0)
            act.wait_ge(s_half, 1)
            for g in range(1, NG):
                root(g)
                count_signs(g - 1)
            for a in range(NG - 1, WG):
                count_signs(a)
            on_request(small[:, 3, 0:J], small[:, 2, 0:J], ACT.Sqrt)
            on_request(factor[:, 5, :], factor[:, 4, :], ACT.Sqrt)
            split(0, G)
            act.wait_ge(s_rows_d, 16)
            act.wait_ge(s_keys_d, 32)
            act.wait_ge(s_eap, 16)
            for h in range(2):
                act.wait_ge(s_run[h], 16)
            act.wait_ge(s_key16, 1)

            def spread_keys(windows_, h):
                act.activation(spread[:, h, :, :], key16[:, 0, windows_].unsqueeze(2).to_broadcast([P, 8, P]),
                               ACT.Copy).then_inc(s_spread, 1)

            for h in range(2):
                spread_keys(slice(h * 8, h * 8 + 8), h)
            windows = A[:, :].rearrange("p (w c) -> p w c", c=J * J)
            with act.Fori(0, WG) as g:
                with act.Fori(0, P // 16) as i:
                    for h in range(2):
                        act.wait_ge(s_amm, g * (P // 8) + i * 2 + (2 + h + 1))
                        act.activation(
                            windows[:, bass.ds(i * 16 + h * 8, 8), bass.ds(g * WC, WC)].rearrange(
                                "p (a w) c -> p a w c", a=2),
                            PSALL[:, 4 + 2 * h:6 + 2 * h, 0:4 * WC].rearrange("p a (w c) -> p a w c", w=4),
                            ACT.Copy).then_inc(s_aev, 1)
                        spread_keys(bass.ds(g * P + i * 16 + (16 + h * 8), 8), h)
            dense(blocks_of(*((0, g) for g in range(NG))))
            for r in range(1, NG + 2):
                dense(blocks_of(*round_groups(r)))
                if r <= NG:
                    root(r - 1)
            edges(0)
            for g in range(NG):
                dense(blocks_of((3, g)))
            edges(1)
            for g in range(NG):
                root(g)
                high(2, g, G)
            split(3, G)
            for g in range(NG):
                root(g)
            split(4, H, PAIR)
            for g in range(NG):
                dense(blocks_of((4, g)))
            split(5, H, top[:, NG + 2:NG + 3])
            for g in range(NG):
                dense(blocks_of((5, g)))

        @block.vector
        def _(dve):
            steps = [0]
            asks = [0]

            def v(instruction):
                steps[0] += 1
                instruction.then_inc(s_v, 1)
                dve.wait_ge(s_v, steps[0])

            def ask(instruction):
                asks[0] += 1
                instruction.then_inc(s_a_in, 1)
                dve.wait_ge(s_a_out, asks[0])

            def per_node(t, n=GR):
                return t.unsqueeze(2).to_broadcast([P, n, D])

            def of(t, g):
                return t[:, g * GR:(g + 1) * GR]

            def scale(out_, in_, by, g):
                return dve.tensor_tensor(out_, in_, per_node(of(by, g)), ALU.mult)

            def to_integer(t):
                v(dve.tensor_scalar(t, t, MAGIC, MAGIC, ALU.add, ALU.subtract))

            def layernorm(g, square):
                xg, hg = group(X, g), group(H, g)
                s0, s1, s2 = (of(stat[:, i, :], g) for i in range(3))
                v(dve.tensor_reduce(s0, xg, AX.X, ALU.add))
                v(dve.scalar_tensor_tensor(hg, per_node(s0), -1.0 / D, xg, ALU.mult, ALU.add))
                v(dve.tensor_tensor(square, hg, hg, ALU.mult))
                v(dve.tensor_reduce(s1, square, AX.X, ALU.add))
                ask(dve.tensor_scalar(s1, s1, 1.0 / D, EPS, ALU.mult, ALU.add))
                v(dve.reciprocal(s0, s2))
                return dve.scalar_tensor_tensor(hg, hg, 0.0, per_node(s0), ALU.max, ALU.mult)

            def low(k, g, source, by=1.0):
                dve.wait_ge(s_high, NG * max(k - 1, 0) + g + 1)
                dve.scalar_tensor_tensor(group(HL, g)[:, :, D:2 * D], group(source, g), by,
                                         group(HL, g)[:, :, 0:D], ALU.mult, ALU.subtract).then_inc(s_split, 1)

            def split(k, source, by=1.0):
                for g in range(NG):
                    low(k, g, source, by)

            def sums(k, g):
                for b in range(g * GR, (g + 1) * GR):
                    dve.wait_ge(s_hmm, J * k + b + 1)
                    dve.tensor_reduce(G[:, b, :], PS[b % 5][:, 0:2 * D].rearrange("p (k d) -> p d k", k=2),
                                      AX.X, ALU.add).then_inc(s_hsum, 1)
                dve.wait_ge(s_hsum, 5 + J * k + (g + 1) * GR)

            def use(k, g, block_step):
                for b in range(g * GR, (g + 1) * GR):
                    dve.wait_ge(s_dmm, at(k, b) + 1)
                    if k in (2, 3):
                        dve.wait_ge(s_root, J * (k - 2) + b + 1)
                    block_step(b).then_inc(s_dep, 1)
                dve.wait_ge(s_dep, group_done(k, g))

            def edges(n, finish):
                dve.wait_ge(s_pickc, 1)
                dve.tensor_reduce(top[:, 0:1], G[:, :, :], AX.XY, ALU.max, apply_absolute_value=True
                                  ).then_inc(s_scale, 1)
                dve.wait_ge(s_scaleT, 2 * n + 1)
                v(dve.tensor_reduce(top[0:1, 0:1], PS[7][0:1, 0:P], AX.X, ALU.max))
                v(dve.tensor_scalar(top[0:1, NG:NG + 1], top[0:1, 0:1], 1e-20, 1.0 / PAIR_TOP, ALU.max, ALU.mult))
                dve.reciprocal(top[0:1, NG + 1:NG + 2], top[0:1, NG:NG + 1]).then_inc(s_scale, 1)
                dve.wait_ge(s_scaleT, 2 * n + 2)
                dve.tensor_copy(top[:, NG + 1:NG + 3], PS[6][:, 0:2]).then_inc(s_scale, 1)
                dve.wait_ge(s_scale, 3 * n + 3)
                for g in range(NG):
                    dve.wait_ge(s_part1, NG * n + g + 1)
                    dve.scalar_tensor_tensor(group(parts, g)[:, :, 1, :], group(G, g), table_scale,
                                             group(parts, g)[:, :, 0, :], ALU.mult, ALU.subtract
                                             ).then_inc(s_parts, 1)

                def one_hots(a, first, last):
                    return dve.tensor_tensor(
                        pick[:, a, first:last, :],
                        own_slot[:, a * P:(a + 1) * P].unsqueeze(1).to_broadcast([P, last - first, P]),
                        slot_id[:, first:last, :], ALU.is_equal)

                dve.wait_ge(s_parts, NG * (n + 1))
                v(dve.memset(running[:, CH - 1, :], -BIG))
                v(dve.memset(carry_scan[:, 0:1], -BIG))
                dve.wait_ge(s_own, n * (NCH + 1) + 1)
                for a in range(PICKS):
                    one_hots(a, 0, J).then_inc(s_pick, 1)
                with dve.Fori(0, NCH) as it:
                    for q in range(NQ):
                        dve.wait_ge(s_msg, it * NQ + (n * NCH * NQ + q + 1 + 2))
                        if q >= SUMMED:
                            gathers = Q if q < NQ - 1 else Q - PICKS
                            dve.wait_ge(s_gat[q], it * (16 * gathers) + 16 * gathers * (n * NCH + 1))
                            if q == NQ - 1:
                                dve.wait_ge(s_picked, it * PICKS + (PICKS * n * NCH + 1 + PICKS))
                            rows = gathered[:, q * Q:(q + 1) * Q, :].rearrange("p t d -> p (t d)")
                            k = gathers * D
                            added = dve.tensor_tensor(rows[:, 0:k], PS[q][:, 0:k], rows[:, 0:k], ALU.add)
                            if q == NQ - 1:
                                added = dve.scalar_tensor_tensor(rows[:, k:Q * D], rows[:, k:Q * D], table_unscale,
                                                                 PS[q][:, k:Q * D], ALU.mult, ALU.add)
                            added.then_inc(s_message, 1)
                        if q % 2 == 0:
                            dve.wait_ge(s_run[q // 2], it * 16 + 16 * (n * NCH + 1))
                        if q >= SUMMED:
                            k = NQ - SUMMED
                            dve.wait_ge(s_message, it * k + (n * NCH * k + k + q - SUMMED + 1))
                        for i in range(Q):
                            t = q * Q + i
                            dve.wait_ge(s_scan, it * CH + (CH + n * T + t))
                            dve.scalar_tensor_tensor(running[:, t, :], running[:, (t - 1) % CH, :],
                                                     reset[:, bass.ds(it * CH + t, 1)],
                                                     PS[q][:, i * D:(i + 1) * D] if q < SUMMED
                                                     else gathered[:, t, :], ALU.add, ALU.max).then_inc(s_scan, 1)
                            a = q - (NQ - PICKS)
                            if a == 0 and i == 0:
                                dve.wait_ge(s_own, it + (n * (NCH + 1) + 2))
                            if a >= 0:
                                piece = one_hots(a, i * J // Q, (i + 1) * J // Q)
                                if i == Q - 1:
                                    piece.then_inc(s_pick, 1)
                        if q < PICKS:
                            dve.wait_ge(s_pmm, it * PICKS + (PICKS * n * NCH + q + 1))
                            dve.tensor_reduce(gathered[:, PICKED + q, :],
                                              PS[6][:, 0:2 * D].rearrange("p (k d) -> p d k", k=2),
                                              AX.X, ALU.add).then_inc(s_picked, 1)
                dve.wait_ge(s_lastT, n + 1)
                dve.tensor_tensor_scan(carry_scan[:, 1:P + 1], carry_reset[0:D, :], PS[6][0:D, 0:P], -BIG,
                                       ALU.add, ALU.max).then_inc(s_carry, 1)
                dve.wait_ge(s_carryT, n + 1)
                dve.wait_ge(s_fs, 16 * (n + 1))
                dve.tensor_tensor(crossing, PS[7][:, 0:D], first_seg, ALU.max).then_inc(s_cross, 1)
                for g in range(NG):
                    dve.wait_ge(s_agg[g], 16 * GR * (n + 1))
                    v(dve.tensor_tensor(group(agg, g), group(agg, g), group(H, g), ALU.add))
                    finish(g)

            def leaky(out_, g):
                return dve.scalar_tensor_tensor(out_, group(agg, g), 0.01, group(agg, g), ALU.mult, ALU.max)

            for signal, count in ((s_aev, 2), (s_hsum, 5), (s_more_sum, 1), (s_message, NQ - SUMMED), (s_picked, 1),
                                  (s_scan, CH), (s_aTc, 2), (s_msg, 2), (s_amm, 2)):
                dve.sem_inc(signal, count)
            dve.memset(X[:, :, :], 0.0).then_inc(s_padx, 1)

            dve.wait_ge(s_dst, 48)
            dve.tensor_copy(dst_f, dst_i).then_inc(s_dstf, 1)
            dve.wait_ge(s_const, 3)
            dve.wait_ge(s_dstf, 1)
            dve.tensor_scalar(diag[:, 0, :], ident[:, :], dst_f[:, 0:1], None, ALU.mult)
            dve.tensor_scalar(diag[:, 1, :], ident[:, :], dst_f[:, T - 1:T], None, ALU.mult).then_inc(s_diag, 1)
            dve.wait_ge(s_src, 48)
            v(dve.tensor_copy(src_f, src_i[:, 0:T]))
            dve.wait_ge(s_bcast, 1)
            firsts = PS[7][:, 0:P]
            row = small[:, 0, :]
            v(dve.tensor_tensor(first_less[:, 0:FIRST, :], firsts.unsqueeze(1).to_broadcast([P, FIRST, P]),
                                node_id[:, 0:J + 1:WN].unsqueeze(2).to_broadcast([P, FIRST, P]), ALU.is_lt))
            v(dve.tensor_reduce(row[:, 0:J + 1:WN], first_less[:, 0:FIRST, :], AX.X, ALU.add))
            v(dve.tensor_scalar(row[:, 0:J + 1:WN], row[:, 0:J + 1:WN], 1.0, 0.0, ALU.subtract, ALU.max))
            dve.tensor_copy(row_i[:, 0:J + 1:WN], row[:, 0:J + 1:WN]).then_inc(s_row_i, 1)
            v(dve.tensor_scalar(src_hi, src_f, 1.0 / J, 0.48, ALU.mult, ALU.subtract))
            to_integer(src_hi)
            v(dve.scalar_tensor_tensor(src_f, src_hi, -float(J), src_f, ALU.mult, ALU.add))
            v(dve.tensor_copy(keys[:, :, 0], src_hi))
            dve.scalar_tensor_tensor(keys[:, :, 1], dst_f, float(J), src_f, ALU.mult, ALU.add).then_inc(s_keys, 1)

            def inner(t):
                return t[:, 0:J].rearrange("p (a r) -> p a r", r=WN)[:, :, 1:WN]

            some = first_less[:, 0:WG * (WN - 1), :].rearrange("p (a r) c -> p a r c", a=WG)
            v(dve.tensor_tensor(some, firsts.unsqueeze(1).unsqueeze(1).to_broadcast([P, WG, WN - 1, P]),
                                inner(node_id).unsqueeze(3).to_broadcast([P, WG, WN - 1, P]), ALU.is_lt))
            v(dve.tensor_reduce(inner(row), some, AX.X, ALU.add))
            v(dve.tensor_scalar(inner(row), inner(row), 1.0, 0.0, ALU.subtract, ALU.max))
            dve.tensor_copy(inner(row_i[:, :]), inner(row)).then_inc(s_row_i, 1)

            def count(j):
                v(dve.tensor_scalar(row_trash, found_rows[:, j, :], node_id[:, j:j + 1], None, ALU.is_lt, ALU.add,
                                    accum_out=small[:, 1, j:j + 1]))

            dve.wait_ge(s_found[0], 16 * FIRST)
            for j in range(0, J + 1, WN):
                count(j)
            some = slice(0, J + 1, WN)
            v(dve.scalar_tensor_tensor(starts[:, some], row[:, some], float(T), small[:, 1, some], ALU.mult, ALU.add))
            v(dve.tensor_tensor(small[:, 3, 0:WG], starts[:, WN:J + 1:WN], starts[:, 0:J:WN], ALU.subtract))
            v(dve.tensor_reduce(top[:, 0:1], small[:, 3, 0:WG], AX.X, ALU.max))
            dve.tensor_copy(win_i[:, :], starts[:, 0:J:WN]).then_inc(s_win_i, 1)

            v(dve.memset(small[:, 3, :], 0.0))
            dve.tensor_scalar(half_off, node_id, -1.0, 0.5, ALU.mult, ALU.add).then_inc(s_half, 1)

            v(dve.memset(reset[:, 0:1], 0.0))
            v(dve.tensor_tensor(reset[:, 1:T], dst_f[:, 1:T], dst_f[:, 0:T - 1], ALU.not_equal))
            v(dve.tensor_scalar(reset[:, :], reset[:, :], -BIG, None, ALU.mult))
            v(dve.memset(carry_reset[:, 0:1], -BIG))
            v(dve.tensor_copy(diag[:, 1, :], PS[7][:, P:2 * P]))
            v(dve.tensor_tensor(carry_reset[:, 1:P], diag[:, 1, 1:P], diag[:, 1, 0:P - 1], ALU.not_equal))
            v(dve.tensor_scalar(carry_reset[:, 1:P], carry_reset[:, 1:P], -BIG, None, ALU.mult))
            one = small[:, 2, 0:1]
            v(dve.tensor_scalar(row_trash, dst_f, dst_f[:, 0:1], None, ALU.is_equal, ALU.add, accum_out=one))
            v(dve.scalar_tensor_tensor(one, one, -1.0, part_edge, ALU.add, ALU.add))
            v(dve.tensor_copy(first_end_i[:, :], one))

            dve.wait_ge(s_x, 32)
            for g in range(NG):
                v(layernorm(g, group(square0, g)))

            dve.wait_ge(s_winT, 1)
            v(dve.memset(key16[:, :, :], 0.0))
            flat = PSALL[:, 0:3, :].rearrange("p a c -> p (a c)")
            v(dve.tensor_copy(key16[:, 0, 0:WG * P], flat[:, 0:WG * P]))
            v(dve.tensor_tensor(key_col, flat[:, WG * P:2 * WG * P], window_base, ALU.subtract))
            dve.tensor_scalar(key16[:, 1, 0:WG * P], key_col, -1.0, float(P - 1), ALU.max, ALU.min
                              ).then_inc(s_key16, 1)
            count_ = top[0:1, 1:2]
            v(dve.tensor_reduce(count_, PS[3][0:1, 0:P], AX.X, ALU.max))
            v(dve.tensor_scalar(count_, count_, 1.0 / P, 0.502, ALU.mult, ALU.subtract))
            v(dve.tensor_scalar(count_, count_, 0.0, None, ALU.max))
            to_integer(count_)
            dve.tensor_copy(rounds_i[:, :], count_).then_inc(s_rounds, 1)
            dve.wait_ge(s_counted, WG * (WN - 1))
            signs = small[:, 3, :]
            v(dve.tensor_scalar(inner(signs), inner(signs), -0.5, T / 2.0, ALU.mult, ALU.add))
            v(dve.scalar_tensor_tensor(inner(starts), inner(row), float(T), inner(signs), ALU.mult, ALU.add))

            deg = small[:, 1, 0:J]
            v(dve.tensor_tensor(deg, starts[:, 1:J + 1], starts[:, 0:J], ALU.subtract))
            v(dve.tensor_scalar(has_edges[:, :], deg, 1.0, None, ALU.min))
            v(dve.tensor_scalar(factor[:, 4, :], deg, 1.0, None, ALU.add))
            v(dve.reciprocal(inv_deg1[:, :], factor[:, 4, :]))
            ask(dve.tensor_scalar(small[:, 2, 0:J], deg, 1.0, None, ALU.max))
            ask(dve.reciprocal(inv_deg[:, :], small[:, 2, 0:J]))
            v(dve.reciprocal(small[:, 1, 0:J], small[:, 3, 0:J]))
            v(dve.reciprocal(small[:, 2, 0:J], factor[:, 5, :]))
            inv_sqrt, inv_sqrt1 = small[:, 1, 0:J], small[:, 2, 0:J]
            for i, (t, by) in enumerate(((inv_sqrt, PAIR), (inv_sqrt, -1.0 / PAIR), (inv_sqrt, -2.0 / PAIR),
                                         (inv_sqrt1, PAIR), (inv_sqrt1, 1.0 / PAIR), (inv_deg[:, :], 1.0 / PAIR))):
                v(dve.tensor_scalar(factor[:, i, :], t, by, None, ALU.mult))

            dve.wait_ge(s_rows_d, 16)
            dve.wait_ge(s_keys_d, 32)
            for g in range(NG):
                scale(group(G, g), group(H, g), factor[:, 0, :], g).then_inc(s_u, 1)
            split(0, G)

            def first_sum(b):
                dve.wait_ge(s_hmm, b + 1)
                dve.tensor_reduce(G[:, b, :], PS[b % 4][:, 0:2 * D].rearrange("p (k d) -> p d k", k=2),
                                  AX.X, ALU.add).then_inc(s_hsum, 1)

            sum_at = {(b // GR + 1) * HALVES + 7 + 3 * (b % GR): b for b in range(J)}
            dve.wait_ge(s_key16, 1)
            for half in range(WG * HALVES):
                h = half % 2
                dve.wait_ge(s_amm, half + 1)
                dve.tensor_tensor(
                    onehot[:, 1, h, :, 0:WC], iota16[:, 0:WC].unsqueeze(1).to_broadcast([P, 8, WC]),
                    key16[:, 1, half * 8:half * 8 + 8].unsqueeze(2).to_broadcast([P, 8, WC]), ALU.is_equal)
                dve.wait_ge(s_spread, half + 1)
                dve.tensor_tensor(onehot[:, 0, h, :, :], iota16.unsqueeze(1).to_broadcast([P, 8, P]),
                                  spread[:, h, :, :], ALU.is_equal).then_inc(s_onehot, 1)
                if half in sum_at:
                    first_sum(sum_at[half])
            for half, b in sum_at.items():
                if half >= WG * HALVES:
                    first_sum(b)

            next_start = stat[:, 0, 0:WG]
            v(dve.tensor_copy(next_start, starts[:, 0:J:WN]))
            dve.wait_ge(s_amm, 2 + WG * P // 8)
            dve.wait_ge(s_spread, WG * P // 8 + 2)
            dve.wait_ge(s_rounds, 1)
            rounds = dve.value_load(rounds_i[0:1, 0:1], min_val=0, max_val=T)
            with dve.If(rounds), dve.Fori(0, rounds) as r:
                taken = [0]

                def more(instruction):
                    taken[0] += 1
                    instruction.then_inc(s_more_v, 1)
                    dve.wait_ge(s_more_v, r * (2 + 2 * WG) + (taken[0] + 1))

                more(dve.tensor_scalar(next_start, next_start, float(P), float(EP), ALU.add, ALU.min))
                dve.tensor_copy(win_i[:, :], next_start).then_inc(s_more_win, 1)
                dve.wait_ge(s_more_T, r + 1)
                more(dve.tensor_copy(key16[:, 0, 0:WG * P], flat[:, 0:WG * P]))
                for g in range(WG):
                    more(dve.scalar_tensor_tensor(more_col, flat[:, (WG + g) * P:(WG + g + 1) * P], float(-g * WC),
                                                  first_column, ALU.add, ALU.subtract))
                    more(dve.tensor_scalar(key16[:, 1, g * P:(g + 1) * P], more_col, -1.0, float(P - 1),
                                           ALU.max, ALU.min))
                dve.sem_inc(s_more_turn, 1)
                for g in range(WG):
                    with dve.Fori(0, P // 8) as i:
                        for k, width in ((1, WC), (0, P)):
                            hot = dve.tensor_tensor(
                                onehot[:, k, 0, :, 0:width],
                                iota16[:, 0:width].unsqueeze(1).to_broadcast([P, 8, width]),
                                key16[:, k, bass.ds(i * 8 + g * P, 8)].unsqueeze(2).to_broadcast([P, 8, width]),
                                ALU.is_equal)
                        hot.then_inc(s_more_onehot, 1)
                        dve.wait_ge(s_more_mm, r * (WG * P // 8) + i + (g * (P // 8) + 1))
                        part = A[:, :].rearrange("p (w c) -> p w c", c=J * J)[
                            :, bass.ds(i * 8, 8), g * WC:(g + 1) * WC].rearrange("p (a w) c -> p a w c", a=2)
                        dve.tensor_tensor(part, part, PSALL[:, 4:6, 0:4 * WC].rearrange("p a (w c) -> p a w c", w=4),
                                          ALU.add).then_inc(s_more_add, 1)
            with dve.If(rounds), dve.Fori(0, J) as b:
                dve.wait_ge(s_more_hmm, b + 1)
                dve.tensor_reduce(G[:, bass.ds(b, 1), :].rearrange("p b d -> p (b d)"),
                                  PS[0][:, 0:2 * D].rearrange("p (k d) -> p d k", k=2),
                                  AX.X, ALU.add).then_inc(s_more_sum, 1)
            with dve.If(rounds):
                dve.wait_ge(s_more_sum, 1 + J)
                dve.sem_inc(s_more_turn, 1)
            dve.sem_inc(s_built, 1)

            dve.wait_ge(s_hsum, 5 + J)
            for g in range(NG):
                scale(group(G, g), group(G, g), factor[:, 1, :], g).then_inc(s_din, 1)
            dve.wait_ge(s_w0, 32)
            dve.tensor_tensor(wdense[0:D, 0, :], wdense[0:D, 0, :], wdense[0:D, 2, :], ALU.subtract
                              ).then_inc(s_w02, 1)
            for g in range(NG):
                dve.wait_ge(s_din, g + 1)
                v(scale(group(HL, g)[:, :, 0:D], group(G, g), factor[:, 0, :], g))
                for j in range(g * GR, (g + 1) * GR):
                    last = dve.scalar_tensor_tensor(HL[:, j, D:2 * D], G[:, j, :], factor[:, 0, j:j + 1],
                                                    HL[:, j, 0:D], ALU.mult, ALU.subtract)
                last.then_inc(s_split, 1)

            e, end_row, crosses = small[:, 1, 0:J], small[:, 2, 0:J], small[:, 3, 0:J]
            v(dve.tensor_scalar(e, starts[:, 1:J + 1], 1.0, 0.0, ALU.subtract, ALU.max))
            v(dve.tensor_scalar(end_row, e, (T - 1) / 2.0, 1.0 / T, ALU.subtract, ALU.mult))
            to_integer(end_row)
            v(dve.scalar_tensor_tensor(crosses, end_row, float(T), starts[:, 0:J], ALU.mult, ALU.is_gt))
            v(dve.tensor_scalar(end_row, end_row, float(EP), None, ALU.add))
            v(dve.tensor_tensor(end_row, end_row, e, ALU.subtract))
            v(dve.tensor_tensor(end_row, end_row, crosses, ALU.mult))
            v(dve.tensor_tensor(e, e, end_row, ALU.add))
            v(dve.tensor_scalar(e, e, ZERO_ROW, None, ALU.subtract))
            v(dve.tensor_tensor(e, e, has_edges[:, :], ALU.mult))
            v(dve.tensor_scalar(e, e, ZERO_ROW, None, ALU.add))
            v(dve.tensor_copy(end_i[:, :], e))

            dve.wait_ge(s_x, 64)

            def layer1_in(g):
                v(dve.scalar_tensor_tensor(group(X, g), group(H, g), 0.0, group(X, g), ALU.max, ALU.add))
                layernorm(g, group(G, g)).then_inc(s_din, 1)

            for r in range(NG + 2):
                if r < NG:
                    sums(1, r)
                    scale(group(G, r), group(G, r), factor[:, 2, :], r).then_inc(s_din, 1)
                if 1 <= r <= NG:
                    use(1, r - 1, lambda b: dve.tensor_tensor(H[:, b, :], product(1, b, 0, D), H[:, b, :], ALU.add))
                if r >= 2:
                    use(2, r - 2, lambda b: dve.tensor_copy(G[:, b, :], product(2, b, 0, D)))
                if 1 <= r <= NG:
                    layer1_in(r - 1)

            dve.wait_ge(s_y, 16 * NG)

            def second_table(g):
                use(3, g, lambda b: dve.tensor_copy(G[:, b, :], product(3, b, 0, D)))

            def layer1_middle(g):
                leaky(group(H, g), g).then_inc(s_din, 1)
                if g:
                    second_table(g - 1)

            edges(0, layer1_middle)
            second_table(NG - 1)
            dve.wait_ge(s_y, 32 * NG)

            def layer2_in(g):
                v(leaky(group(G, g), g))
                v(dve.tensor_tensor(group(X, g), group(X, g), group(G, g), ALU.add))
                v(layernorm(g, group(G, g)))
                scale(group(G, g), group(H, g), factor[:, 3, :], g).then_inc(s_u, 1)
                if g:
                    low(2, g - 1, G)

            edges(1, layer2_in)
            low(2, NG - 1, G)

            def looped(g):
                v(scale(group(H, g), group(H, g), inv_deg1, g))
                v(scale(group(G, g), group(G, g), factor[:, 4, :], g))
                v(dve.tensor_tensor(group(H, g), group(H, g), group(G, g), ALU.add))

            def hop2_out(g):
                looped(g)
                scale(group(G, g), group(H, g), factor[:, 3, :], g).then_inc(s_u, 1)

            def hop3_out(g):
                looped(g)
                v(dve.tensor_tensor(group(X, g), group(X, g), group(H, g), ALU.add))
                layernorm(g, group(G, g)).then_inc(s_u, 1)

            for g in range(NG):
                sums(2, g)
                hop2_out(g)
            split(3, G)
            for g in range(NG):
                sums(3, g)
                hop3_out(g)

            split(4, H, PAIR)
            for r in range(NG + 1):
                if r < NG:
                    sums(4, r)
                    scale(group(G, r), group(G, r), factor[:, 5, :], r).then_inc(s_din, 1)
                if r:
                    use(4, r - 1, lambda b: dve.tensor_scalar(H[:, b, :], product(4, b, 0, D), 0.0, None, ALU.max))
                    v(dve.tensor_reduce(top[:, r - 1:r], group(H, r - 1), AX.XY, ALU.max))
            v(dve.memset(ones_row, 1.0))
            dve.tensor_reduce(top[:, NG:NG + 1], top[:, 0:NG], AX.X, ALU.max).then_inc(s_top, 1)
            dve.wait_ge(s_topT, 1)
            v(dve.tensor_reduce(top[0:1, 0:1], PS[7][0:1, 0:P], AX.X, ALU.max))
            v(dve.tensor_scalar(top[0:1, NG:NG + 1], top[0:1, 0:1], 1e-20, 1.0 / PAIR_TOP, ALU.max, ALU.mult))
            dve.reciprocal(top[0:1, NG + 1:NG + 2], top[0:1, NG:NG + 1]).then_inc(s_top, 1)
            dve.wait_ge(s_topT, 2)
            v(dve.tensor_copy(top[:, NG + 1:NG + 3], PS[6][:, 0:2]))
            dve.tensor_scalar(factor[:, 5, :], inv_deg[:, :], top[:, NG + 1:NG + 2], None, ALU.mult
                              ).then_inc(s_u, NG)
            split(5, H, top[:, NG + 2:NG + 3])
            for r in range(NG + 1):
                if r < NG:
                    sums(5, r)
                    scale(group(G, r), group(G, r), factor[:, 5, :], r).then_inc(s_din, 1)
                if r:
                    use(5, r - 1, lambda b: dve.tensor_tensor(X[:, b, :], product(5, b, 0, D), X[:, b, :], ALU.add))


_INS = ['x', 'src', 'dst', 'edge_attr_32', 'L0_gnn_W', 'L0_gnn_b', 'L1_gnn_W1_msg', 'L1_gnn_W1_edge',
        'L1_gnn_W1_root', 'L1_gnn_b1', 'L1_gnn_W2_msg', 'L1_gnn_W2_edge', 'L1_gnn_W2_root', 'L1_gnn_b2',
        'L3_gnn_W_self1', 'L3_gnn_W_neigh1', 'L3_gnn_b1', 'L3_gnn_W_self2', 'L3_gnn_W_neigh2', 'L3_gnn_b2']


def kernel(**inputs):
    import numpy as _np
    import concourse.bacc as _bacc
    from concourse import mybir as _mybir
    from concourse.bass_utils import run_bass_kernel_spmd as _run

    nc = _bacc.Bacc("TRN2", target_bir_lowering=False, num_devices=1)
    arrays, args = {}, []
    for name in _INS:
        a = _np.ascontiguousarray(inputs[name])
        arrays[f"in_{name}"] = a
        args.append(nc.dram_tensor(f"in_{name}", a.shape, _mybir.dt.from_np(a.dtype), kind="ExternalInput").ap())
    out = nc.dram_tensor("out_x", (N, D), F32, kind="ExternalOutput").ap()
    gnn_kernel(nc, *args, out)
    r = _run(nc, [arrays], core_ids=[0])
    return r.results[0]["out_x"]
```
